# Optimizing a Trainium2 kernel written in Bass

```python
import numpy as np
import jax
import jax.numpy as jnp

def _softmax(x, axis=-1):
    return jax.nn.softmax(x, axis=axis)

def _gelu(x):
    return jax.nn.gelu(x, approximate=True)

def _silu(x):
    return jax.nn.silu(x)

def _sigmoid(x):
    return jax.nn.sigmoid(x)

def _layernorm(x, axis=-1, eps=1e-05):
    m = jnp.mean(x, axis=axis, keepdims=True)
    v = jnp.var(x, axis=axis, keepdims=True)
    return (x - m) / jnp.sqrt(v + eps)

def _scatter_add(tgt, idx, src, axis=0):
    return tgt.at[idx].add(src)

def _segment_sum(src, seg, n):
    return jax.ops.segment_sum(src, seg, n)
kernel_name = 'mk_cond_resid_d2_seqx_r4_e79b26'

def setup_inputs(seed: int=0):
    np.random.seed(seed)
    _w = jnp.asarray

    def _rec_inputs():
        import jax
        import jax.numpy as jnp
        _rk = jax.random.key(seed)
        x = -0.0003929 + 0.9999 * jax.random.normal(jax.random.fold_in(_rk, 1), (2, 1024, 256), jnp.float32)
        _lenS = 1024 - jax.random.randint(jax.random.fold_in(_rk, 7), (2,), 0, max(1, 1024 // 4) + 1, jnp.int32)
        _lenS2 = 1024 - jax.random.randint(jax.random.fold_in(_rk, 8), (2,), 0, max(1, 1024 // 4) + 1, jnp.int32)
        cond_1024 = 0.00513981 + 1.0024 * jax.random.normal(jax.random.fold_in(_rk, 11), (2, 256), jnp.float32)
        return (x, cond_1024)
    x, cond_1024 = _rec_inputs()

    def _L0_cond_setup():
        import jax, jax.numpy as jnp
        import numpy as np
        EMBED = 256
        HID = 256
        B, T = (32, 128)

        def _gru_layer(x, Wih, Whh, bih, bhh):
            H = Whh.shape[1]
            xg = jnp.einsum('bti,gi->tbg', x, Wih) + bih

            def step(h, xt):
                hg = h @ Whh.T + bhh
                xr, xz, xn = jnp.split(xt, 3, axis=-1)
                hr, hz, hn = jnp.split(hg, 3, axis=-1)
                r = jax.nn.sigmoid(xr + hr)
                z = jax.nn.sigmoid(xz + hz)
                n = jnp.tanh(xn + r * hn)
                h_new = (1.0 - z) * n + z * h
                return (h_new, h_new)
            h0 = jnp.zeros((x.shape[0], H), dtype=x.dtype)
            _, ys = jax.lax.scan(step, h0, xg)
            return jnp.transpose(ys, (1, 0, 2))
        key = jax.random.key(seed)
        ks = jax.random.split(key, 16)
        s_in = 1.0 / np.sqrt(EMBED)
        s_h = 1.0 / np.sqrt(HID)
        return {'x': jax.random.normal(ks[0], (B, T, EMBED), jnp.float32), 'context': jax.random.normal(ks[1], (B, HID), jnp.float32), 'W_in': jax.random.uniform(ks[2], (HID, EMBED), jnp.float32, -s_in, s_in), 'b_in': jax.random.uniform(ks[3], (HID,), jnp.float32, -s_in, s_in), 'Wih0': jax.random.uniform(ks[4], (3 * HID, HID), jnp.float32, -s_h, s_h), 'Whh0': jax.random.uniform(ks[5], (3 * HID, HID), jnp.float32, -s_h, s_h), 'bih0': jax.random.uniform(ks[6], (3 * HID,), jnp.float32, -s_h, s_h), 'bhh0': jax.random.uniform(ks[7], (3 * HID,), jnp.float32, -s_h, s_h), 'Wih1': jax.random.uniform(ks[8], (3 * HID, HID), jnp.float32, -s_h, s_h), 'Whh1': jax.random.uniform(ks[9], (3 * HID, HID), jnp.float32, -s_h, s_h), 'bih1': jax.random.uniform(ks[10], (3 * HID,), jnp.float32, -s_h, s_h), 'bhh1': jax.random.uniform(ks[11], (3 * HID,), jnp.float32, -s_h, s_h), 'W_out': jax.random.uniform(ks[12], (EMBED, HID), jnp.float32, -s_h, s_h), 'b_out': jax.random.uniform(ks[13], (EMBED,), jnp.float32, -s_h, s_h), 'W_gate': jax.random.uniform(ks[14], (HID, HID), jnp.float32, -s_h, s_h), 'b_gate': jax.random.uniform(ks[15], (HID,), jnp.float32, -s_h, s_h)}
    _L0_cond_all = _L0_cond_setup()
    _L0_cond_in = {k: v for k, v in _L0_cond_all.items() if k in ('W_in', 'b_in', 'Wih0', 'Whh0', 'bih0', 'bhh0', 'Wih1', 'Whh1', 'bih1', 'bhh1', 'W_out', 'b_out', 'W_gate', 'b_gate')}
    del _L0_cond_all

    def _L1_cond_setup():
        import jax, jax.numpy as jnp
        import numpy as np
        D, HS, HE, E, K = (256, 512, 256, 8, 2)
        B, T = (4, 256)
        N_SHARED = 1
        key = jax.random.key(seed)
        ks = jax.random.split(key, 9)
        g = lambda k, shape, s: jax.random.normal(k, shape, jnp.float32) * s
        return {'x': g(ks[0], (B, T, D), 1.0), 't_emb': g(ks[1], (B, D), 1.0), 'router_W': g(ks[2], (2 * D, E), 0.01), 'router_bias': jnp.zeros((E,), jnp.float32), 'w1': g(ks[3], (D, HS), 0.02), 'w3': g(ks[4], (D, HS), 0.02), 'w2': g(ks[5], (HS, D), 0.02), 'W1e': g(ks[6], (E, D, HE), 0.02), 'W2e': g(ks[7], (E, HE, D), 0.02)}
    _L1_cond_all = _L1_cond_setup()
    _L1_cond_in = {k: v for k, v in _L1_cond_all.items() if k in ('router_W', 'router_bias', 'w1', 'w3', 'w2', 'W1e', 'W2e')}
    del _L1_cond_all
    return {'x': x, 'cond_1024': cond_1024, 'L0_cond_W_in': _L0_cond_in['W_in'], 'L0_cond_b_in': _L0_cond_in['b_in'], 'L0_cond_Wih0': _L0_cond_in['Wih0'], 'L0_cond_Whh0': _L0_cond_in['Whh0'], 'L0_cond_bih0': _L0_cond_in['bih0'], 'L0_cond_bhh0': _L0_cond_in['bhh0'], 'L0_cond_Wih1': _L0_cond_in['Wih1'], 'L0_cond_Whh1': _L0_cond_in['Whh1'], 'L0_cond_bih1': _L0_cond_in['bih1'], 'L0_cond_bhh1': _L0_cond_in['bhh1'], 'L0_cond_W_out': _L0_cond_in['W_out'], 'L0_cond_b_out': _L0_cond_in['b_out'], 'L0_cond_W_gate': _L0_cond_in['W_gate'], 'L0_cond_b_gate': _L0_cond_in['b_gate'], 'L1_cond_router_W': _L1_cond_in['router_W'], 'L1_cond_router_bias': _L1_cond_in['router_bias'], 'L1_cond_w1': _L1_cond_in['w1'], 'L1_cond_w3': _L1_cond_in['w3'], 'L1_cond_w2': _L1_cond_in['w2'], 'L1_cond_W1e': _L1_cond_in['W1e'], 'L1_cond_W2e': _L1_cond_in['W2e']}

def reference(x, cond_1024, L0_cond_W_in, L0_cond_b_in, L0_cond_Wih0, L0_cond_Whh0, L0_cond_bih0, L0_cond_bhh0, L0_cond_Wih1, L0_cond_Whh1, L0_cond_bih1, L0_cond_bhh1, L0_cond_W_out, L0_cond_b_out, L0_cond_W_gate, L0_cond_b_gate, L1_cond_router_W, L1_cond_router_bias, L1_cond_w1, L1_cond_w3, L1_cond_w2, L1_cond_W1e, L1_cond_W2e):
    import jax
    import jax.numpy as jnp

    def _L0_cond_ref(x, context, W_in, b_in, Wih0, Whh0, bih0, bhh0, Wih1, Whh1, bih1, bhh1, W_out, b_out, W_gate, b_gate):
        import jax, jax.numpy as jnp
        import numpy as np
        EMBED = 256
        HID = 256
        B, T = (32, 128)

        def _gru_layer(x, Wih, Whh, bih, bhh):
            H = Whh.shape[1]
            xg = jnp.einsum('bti,gi->tbg', x, Wih) + bih

            def step(h, xt):
                hg = h @ Whh.T + bhh
                xr, xz, xn = jnp.split(xt, 3, axis=-1)
                hr, hz, hn = jnp.split(hg, 3, axis=-1)
                r = jax.nn.sigmoid(xr + hr)
                z = jax.nn.sigmoid(xz + hz)
                n = jnp.tanh(xn + r * hn)
                h_new = (1.0 - z) * n + z * h
                return (h_new, h_new)
            h0 = jnp.zeros((x.shape[0], H), dtype=x.dtype)
            _, ys = jax.lax.scan(step, h0, xg)
            return jnp.transpose(ys, (1, 0, 2))
        ctx = context[:, None, :]
        mixed = jnp.tanh(jnp.einsum('bte,he->bth', x, W_in) + b_in + ctx)
        h1 = _gru_layer(mixed, Wih0, Whh0, bih0, bhh0)
        h2 = _gru_layer(h1, Wih1, Whh1, bih1, bhh1)
        gate = jax.nn.sigmoid(jnp.einsum('bh,gh->bg', context, W_gate) + b_gate)
        gated = gate[:, None, :] * h2 + h2
        return jnp.einsum('bth,eh->bte', gated, W_out) + b_out

    def _L1_cond_ref(x, t_emb, router_W, router_bias, w1, w3, w2, W1e, W2e):
        import jax, jax.numpy as jnp
        import numpy as np
        D, HS, HE, E, K = (256, 512, 256, 8, 2)
        B, T = (4, 256)
        N_SHARED = 1
        Bb, Tt, C = x.shape
        xf = x.reshape(-1, C)
        tf = jnp.broadcast_to(t_emb[:, None, :], (Bb, Tt, C)).reshape(-1, C)
        N = xf.shape[0]
        shared = jax.nn.silu(xf @ w1) * (xf @ w3) @ w2
        s = jax.nn.sigmoid((jnp.concatenate([xf, tf], axis=-1) @ router_W).astype(jnp.float32))
        sel_scores = s + router_bias
        _, topk_idx = jax.lax.top_k(sel_scores, K)
        s_sel = jnp.take_along_axis(s, topk_idx, axis=1)
        denom = s_sel.sum(axis=1, keepdims=True)
        gates = jnp.where(denom > 1e-09, s_sel / (denom + 1e-09), 1.0 / K).astype(x.dtype)
        combine = jnp.zeros((N, E), x.dtype).at[jnp.arange(N)[:, None], topk_idx].add(gates)
        h = jax.nn.gelu(jnp.einsum('nc,ech->enh', xf, W1e), approximate=False)
        y = jnp.einsum('enh,ehc->enc', h, W2e)
        routed = jnp.einsum('ne,enc->nc', combine, y)
        return ((shared + routed) / (N_SHARED + K)).reshape(Bb, Tt, C)
    x = x + _L0_cond_ref(x, cond_1024, L0_cond_W_in, L0_cond_b_in, L0_cond_Wih0, L0_cond_Whh0, L0_cond_bih0, L0_cond_bhh0, L0_cond_Wih1, L0_cond_Whh1, L0_cond_bih1, L0_cond_bhh1, L0_cond_W_out, L0_cond_b_out, L0_cond_W_gate, L0_cond_b_gate)
    x = x + _L1_cond_ref(x, cond_1024, L1_cond_router_W, L1_cond_router_bias, L1_cond_w1, L1_cond_w3, L1_cond_w2, L1_cond_W1e, L1_cond_W2e)
    return x

_drawn_inputs = setup_inputs


def setup_inputs(seed=0):
    import zlib

    import numpy as np

    out = dict(_drawn_inputs(seed))
    spreads = {'L1_cond_router_bias': (0.0, 0.587)}
    factors = {'L0_cond_b_in': 8.0,
     'L0_cond_bih0': 3.219,
     'L0_cond_bhh0': 8.0,
     'L0_cond_bhh1': 3.757,
     'L0_cond_W_gate': 3.904,
     'L0_cond_b_gate': 60.505,
     'L1_cond_router_W': 8.0,
     'L1_cond_w1': 7.059,
     'L1_cond_w3': 6.929,
     'L1_cond_w2': 6.919,
     'L1_cond_W1e': 4.468,
     'L1_cond_W2e': 4.341}
    for name, (base, spread) in spreads.items():
        noise = np.random.default_rng([zlib.crc32(name.encode()), seed]).standard_normal(out[name].shape)
        drawn = base * np.exp(spread * noise) if base else spread * noise
        out[name] = jnp.asarray(drawn.astype(out[name].dtype))
    for name, factor in factors.items():
        out[name] = (out[name] * factor).astype(out[name].dtype)
    return out
```

```python
from contextlib import ExitStack

import concourse.bass as bass
from concourse import mybir
from concourse.alu_op_type import AluOpType as ALU

ACT = mybir.ActivationFunctionType
AX = mybir.AxisListType
F32 = mybir.dt.float32

P = 128
B, T, D = 2, 1024, 256
KT = D // P
NQ = 4
U = D // NQ
UB = U // 32
NGATE = 4
CH = 16
ROWS = CH * B
BODY = 2 * CH
NBODY = T // BODY
LAG = CH + 4
PITCH = ROWS * 4
DIAG = PITCH + B * 4
HS, E, HE = 512, 8, 256
TB = 512
NTB = B * T // TB
SH, EX = HS // P, E * HE // P


class Order:

    def __init__(self, names):
        self.value = {n: i + 1 for i, n in enumerate(names)}

    def at(self, name):
        return self.value[name]


DVE_STEP = ("r_t", "hnz_t", "pre_n", "zh", "h")
ACT_STEP = ("r", "z", "omz", "n")


def dve_at(j, what):
    return len(DVE_STEP) * j + DVE_STEP.index(what) + 1


def act_at(j, what):
    return len(ACT_STEP) * j + ACT_STEP.index(what) + 1


def gru_moe_kernel(nc, a, out):
    with ExitStack() as ctx:
        def sb(name, *shape):
            return ctx.enter_context(nc.sbuf_tensor(name, list(shape), F32))

        def sem(name):
            return ctx.enter_context(nc.semaphore(name))

        w_in = sb("w_in", P, KT, D)
        w_x = [sb(f"w_x{l}", P, KT, NQ, 3 * U) for l in range(2)]
        w_h = [sb(f"w_h{l}", P, KT, NQ, 3 * U) for l in range(2)]
        w_b = [sb(f"w_b{l}", P, NQ, NGATE * U) for l in range(2)]
        w_out = sb("w_out", P, KT, D)
        w_gate = sb("w_gate", P, KT, D)
        w_r = sb("w_r", P, 2 * KT, E)
        w_1 = sb("w_1", P, KT, HS)
        w_3 = sb("w_3", P, KT, HS)
        w_2 = sb("w_2", P, SH, D)
        w_1e = sb("w_1e", P, E, KT, HE)
        w_2e = sb("w_2e", P, E, KT, D)
        b_in = sb("b_in", P, KT)
        b_out = sb("b_out", P, KT)
        b_gate = sb("b_gate", P, KT)
        b_r = sb("b_r", E, 1)
        cond = sb("cond", P, KT, B)
        ones = sb("ones", P, ROWS)
        x_t = sb("x_t", P, KT, T * B)
        mixed = sb("mixed", P, KT, T * B + ROWS)
        hist = sb("hist", P, KT, ROWS + T * B)
        in_bias = sb("in_bias", P, KT, B)
        gate1 = sb("gate1", P, KT, B)
        stage = [sb(f"stage{l}", P, KT, ROWS) for l in range(2)]
        slots = [sb(f"slots{l}", P, CH * DIAG) for l in range(2)]
        r_pre = [sb(f"r_pre{l}", P, ROWS, UB) for l in range(2)]
        hnz = [[sb(f"hnz{l}_{p}", P, 2, ROWS, UB, 2) for p in range(2)] for l in range(2)]
        f_r = [sb(f"f_r{l}", P, B * UB, 2) for l in range(2)]
        v_n = [sb(f"v_n{l}", P, B * UB, 2) for l in range(2)]
        f_z = [sb(f"f_z{l}", P, B * UB, 2) for l in range(2)]
        t_h = [sb(f"t_h{l}", P, B * UB, 2) for l in range(2)]
        z_s = [sb(f"z_s{l}", P, B * UB) for l in range(2)]

        banks = [ctx.enter_context(nc.psum_tensor(f"bank{i}", [P, TB], F32)) for i in range(8)]
        gates = [[banks[2 * l + p] for p in range(2)] for l in range(2)]

        s_ld = sem("s_ld")
        s_ld2 = sem("s_ld2")
        s_set = sem("s_set")
        s_bias = sem("s_bias")
        s_pick = sem("s_pick")
        s_tail = sem("s_tail")
        s_mps = sem("s_mps")
        s_mix = sem("s_mix")
        s_stg = sem("s_stg")
        s_x0 = sem("s_x0")
        s_hist = sem("s_hist")
        KINDS = ("pe", "dve", "act", "pool", "x", "xn", "go")
        sets = [[{k: sem(f"s_{k}{l}_{p}") for k in KINDS} for p in range(2)] for l in range(2)]

        def set_range(l, p):
            nums = [s.num for s in sets[l][p].values()]
            assert nums == list(range(nums[0], nums[0] + len(nums)))
            return range(nums[0], nums[0] + len(nums))

        c_pe, c_act, c_dve, c_out, c_go = (sem(f"c_{n}") for n in ("pe", "act", "dve", "out", "go"))
        assert [c.num for c in (c_pe, c_act, c_dve, c_out)] == list(range(c_pe.num, c_pe.num + 4))

        first_loads = [(w_in, "w_in"), (b_in, "b_in"), (cond, "cond"), (x_t, "x_t"),
                       (w_x[0], "w_x0"), (w_h[0], "w_h0"), (w_x[1], "w_x1"), (w_h[1], "w_h1")]
        late_loads = [(w_out, "w_out"), (w_gate, "w_gate"), (w_r, "w_r"), (w_1, "w_1"), (w_3, "w_3"), (w_2, "w_2"),
                      (w_1e, "w_1e"), (w_2e, "w_2e"), (b_out, "b_out"), (b_gate, "b_gate"), (b_r, "b_r")]
        NSET = 5 + 2 * 5

        def slot_state(l, j):
            return slots[l][:, j * DIAG:j * DIAG + B * 4].rearrange("p (c e) -> p c e", e=2)

        def slot_tile(l, j, kt):
            at = j * PITCH + kt * 2 + 1
            return slots[l][:, at:at + (ROWS - 1) * 4 + 1:4]

        def schedule(s0, n):
            for s in range(s0, s0 + n):
                yield s, (s if s < T else None), (s - LAG if 0 <= s - LAG < T else None)

        def project(pe, l, p, piece, last=None):
            ps = gates[l][p]
            for g in range(NQ):
                rows = ps[32 * g:32 * g + 32, :]
                if piece == 0:
                    mm = pe.matmul(rows[:, 0:NGATE * U], ones[:, :], w_b[l][:, g, :], start=True, stop=False,
                                   tile_position=(0, 32 * g), skip_group_check=True)
                else:
                    mm = pe.matmul(rows[:, U:NGATE * U], stage[l][:, piece - 1, :], w_x[l][:, piece - 1, g, :],
                                   start=False, stop=False, tile_position=(0, 32 * g), skip_group_check=True)
            if last is not None:
                mm.then_inc(last, 1)

        def recur(pe, l, t):
            p, j = t // CH % 2, t % CH
            s = sets[l][p]
            if j == CH - 1 and t < T - 1:
                pe.wait_ge(s["go"], 1)
            if j == 0:
                pe.wait_ge(sets[l][1 - p]["xn"], 1)
            if j:
                pe.wait_ge(s["dve"], dve_at(j - 1, "h"))
            elif t >= CH:
                pe.wait_ge(sets[l][1 - p]["dve"], dve_at(CH - 1, "h"))
            for kt in range(KT):
                for g in range(NQ):
                    mm = pe.matmul(gates[l][p][32 * g:32 * g + 32, 0:3 * U], slot_tile(l, j, kt), w_h[l][:, kt, g, :],
                                   start=False, stop=False, tile_position=(0, 32 * g), skip_group_check=True)
            mm.then_inc(s["pe"], 1)

        def pe_slots(pe, s0, n):
            for s, t0, t1 in schedule(s0, n):
                c, j = divmod(s, CH)
                p = c % 2
                if t0 is not None:
                    recur(pe, 0, t0)
                if CH <= s < T + CH and j < 3:
                    if j == 0:
                        pe.wait_ge(sets[0][p]["pool"], 1)
                    project(pe, 1, 1 - p, j, sets[1][p]["x"] if j == 2 else None)
                if t0 is not None and j in (6, 8, 10):
                    if j == 6:
                        pe.wait_ge(sets[0][p]["pool"], 2)
                    project(pe, 0, 1 - p, (j - 6) // 2, sets[0][p]["x"] if j == 10 else None)
                if t1 is not None:
                    recur(pe, 1, t1)

        def blocks(ap):
            return ap.rearrange("p (b i) -> p b i", i=32)

        def turn_xn(v, l, p):
            v.transpose(hnz[l][p][:, 0, :, :, 1].rearrange("p i b -> p b i"), blocks(gates[l][p][:, 3 * U:4 * U]))\
                .then_inc(sets[l][1 - p]["xn"], 1)

        def dve_head(v, l, t):
            p, j = t // CH % 2, t % CH
            s = sets[l][p]
            if j == 0:
                v.wait_ge(sets[l][1 - p]["xn"], 1)
            if j == CH - 1 and t < T - 1:
                v.wait_ge(s["go"], 1)
            v.wait_ge(s["pe"], j + 1)
            v.transpose(r_pre[l][:].rearrange("p i b -> p b i"), blocks(gates[l][p][:, 2 * U:3 * U])).then_inc(s["dve"], 1)

        def dve_pre(v, l, t):
            p, j = t // CH % 2, t % CH
            s = sets[l][p]
            v.transpose(hnz[l][p][:].rearrange("p g i b e -> p e g b i")[:, 0],
                        gates[l][p][:, 0:2 * U].rearrange("p (g b i) -> p g b i", g=2, i=32)).then_inc(s["dve"], 1)
            v.wait_ge(s["dve"], dve_at(j, "hnz_t"))
            v.wait_ge(s["act"], act_at(j, "r"))
            pairs = hnz[l][p][:, 0, B * j:B * j + B].rearrange("p i b e -> p (i b e)")
            v.tensor_tensor_scan(flat(v_n[l]), flat(f_r[l]), pairs, 0.0, ALU.mult, ALU.add).then_inc(s["dve"], 1)

        def flat(t):
            return t[:].rearrange("p c e -> p (c e)")

        def dve_zh(v, l, t):
            p, j = t // CH % 2, t % CH
            s = sets[l][p]
            v.wait_ge(s["act"], act_at(j, "z"))
            v.tensor_tensor(t_h[l][:, :, 1], z_s[l][:], slot_state(l, j)[:, :, 1], ALU.mult).then_inc(s["dve"], 1)

        def dve_h(v, l, t):
            p, j = t // CH % 2, t % CH
            s = sets[l][p]
            v.wait_ge(s["dve"], dve_at(j, "zh"))
            if j == 0:
                v.wait_ge(s["pool"], 1)
            v.wait_ge(s["act"], act_at(j, "n"))
            v.tensor_tensor_scan(slot_state(l, (j + 1) % CH).rearrange("p c e -> p (c e)"), flat(f_z[l]), flat(t_h[l]),
                                 0.0, ALU.mult, ALU.add).then_inc(s["dve"], 1)

        def dve_slots(v, s0, n, tail=True):
            for s, t0, t1 in schedule(s0, n):
                c, j = divmod(s, CH)
                p = c % 2
                before = t1 - 1 if t1 else None if t1 == 0 or s < LAG else T - 1
                if t0 is not None:
                    dve_head(v, 0, t0)
                if before is not None:
                    dve_h(v, 1, before)
                if t0 is not None:
                    dve_pre(v, 0, t0)
                    dve_zh(v, 0, t0)
                    if j == 12:
                        v.wait_ge(sets[0][p]["x"], 1)
                        turn_xn(v, 0, 1 - p)
                if CH <= s < T + CH and j == 3:
                    v.wait_ge(sets[1][p]["x"], 1)
                    turn_xn(v, 1, 1 - p)
                if t1 is not None:
                    dve_head(v, 1, t1)
                if t0 is not None:
                    dve_h(v, 0, t0)
                if t1 is not None:
                    dve_pre(v, 1, t1)
                    dve_zh(v, 1, t1)

        def act_step(act, l, t):
            p, j = t // CH % 2, t % CH
            s = sets[l][p]
            if j == CH - 1 and t < T - 1:
                act.wait_ge(s["go"], 1)
            act.wait_ge(s["dve"], dve_at(j, "r_t"))
            own = r_pre[l][:, B * j:B * j + B, :].rearrange("p i b -> p (i b)")
            act.activation(f_r[l][:, :, 1], own, ACT.Sigmoid).then_inc(s["act"], 1)
            act.wait_ge(s["dve"], dve_at(j, "hnz_t"))
            own = hnz[l][p][:, 1, B * j:B * j + B, :, 0].rearrange("p i b -> p (i b)")
            act.activation(z_s[l][:], own, ACT.Sigmoid).then_inc(s["act"], 1)
            act.activation(f_z[l][:, :, 1], own, ACT.Sigmoid, scale=-1.0).then_inc(s["act"], 1)
            act.wait_ge(s["dve"], dve_at(j, "pre_n"))
            act.activation(t_h[l][:, :, 0], v_n[l][:, :, 1], ACT.Tanh).then_inc(s["act"], 1)

        def act_slots(act, s0, n):
            for s, t0, t1 in schedule(s0, n):
                if t0 is not None:
                    act_step(act, 0, t0)
                if t1 is not None:
                    act_step(act, 1, t1)

        def read_out(pool, l, dst, done):
            by = slots[l][:].rearrange("p (j r) -> p j r", r=DIAG)
            view = dst.rearrange("p k (j b) -> p k j b", b=B)
            for kt in range(KT):
                own = by[:, :, 0:B * 4].rearrange("p j (b k e) -> p j b k e", b=B, e=2)[:, :, :, kt, 1]
                pool.tensor_copy(view[:, kt, 0:CH - 1], own[:, 1:CH])
                last = pool.tensor_copy(view[:, kt, CH - 1], own[:, 0])
            last.then_inc(done, 1)

        def pool_slots(pool, s0, n, where):
            for s, t0, t1 in schedule(s0, n):
                c, j = divmod(s, CH)
                p = c % 2
                if j == 0 and s <= T:
                    if s >= CH:
                        pool.wait_ge(sets[0][1 - p]["go"], 1)
                        pool.wait_ge(sets[0][1 - p]["dve"], dve_at(CH - 1, "h"))
                    read_out(pool, 0, stage[1][:], sets[0][p]["pool"])
                    if t0 is not None:
                        pool.tensor_copy(stage[0][:], mixed[:, :, where(c + 1)]).then_inc(sets[0][p]["pool"], 1)
                if t1 is not None and t1 % CH == 0:
                    cb = t1 // CH
                    pb = cb % 2
                    if t1 >= CH:
                        pool.wait_ge(sets[1][1 - pb]["go"], 1)
                        pool.wait_ge(sets[1][1 - pb]["dve"], dve_at(CH - 1, "h"))
                    read_out(pool, 1, hist[:, :, where(cb)], sets[1][pb]["pool"])

        def sp_slots(sp, s0, n):
            for s, t0, t1 in schedule(s0, n):
                for l, t in ((0, t0), (1, t1)):
                    if t is not None and t % CH == 0:
                        p = t // CH % 2
                        now = sets[l][p]
                        for k in ("pe", "dve", "act"):
                            sp.wait_ge(now[k], 1)
                        sp.wait_ge(now["pool"], 2 - l)
                        sp.sem_clear(set_range(l, 1 - p))
                        sp.sem_inc(now["go"], 1)

        UNITS = [("s", u) for u in range(SH)] + [("e", u) for u in range(EX)]
        H_BANKS = [banks[i] for i in (2, 3, 4, 5)]
        ACC = [banks[0], banks[1]]
        C_BANKS = [banks[6], banks[7]]

        gated = sb("gated", P, KT, TB)
        x2 = sb("x2", P, KT, TB)
        y = sb("y", P, KT, TB)
        scores = sb("scores", 32, 2, TB)
        by_tok = sb("by_tok", 32, 2, TB // 32, 32)
        gt = sb("gt", 32, TB // 32, E, E)
        ge = sb("ge", 32, TB // 32, E, E)
        lower = sb("lower", 32, E, E)
        rank = sb("rank", 32, TB // 32, E)
        mask = sb("mask", 32, TB // 32, E)
        sel = sb("sel", 32, TB // 32, E)
        denom = sb("denom", 32, TB // 32)
        big = sb("big", 32, TB // 32)
        recip = sb("recip", 32, TB // 32)
        tie = sb("tie", 32, TB // 32)
        comb = sb("comb", 32, TB // 32, 32)
        comb_t = sb("comb_t", 32, TB)
        pick = sb("pick", 32, E, P)
        act_t = [sb(f"act_t{i}", P, TB) for i in range(2)]
        mid = [sb(f"mid{i}", P, TB) for i in range(2)]
        hid = [sb(f"hid{i}", P, TB) for i in range(3)]
        r_bias = sb("r_bias", E, B)
        gsig = sb("gsig", P, KT, B)

        pe_order = Order(["out0", "out1", "route"] + [("up", u) for u in range(SH + EX)][:2]
                         + sum([[("up", u), ("down", u - 2)] for u in range(2, SH + EX)], [])
                         + [("down", SH + EX - 2), ("down", SH + EX - 1)])
        act_order = Order(["score0", "score1"] + [("act", u) for u in range(SH + EX)])
        DVE_ROUTE = ["gated", "x20", "x21", "sel_s", "tok0", "tok1", "gt", "ge", "d", "dl", "rk", "rank", "mask", "sel",
                     "denom", "big", "dplus", "recip", "r_big", "tie", "w_sel", "w_tie", "comb", "comb_t"]
        dve_names = ["gated", "x20", "x21"]
        for u in range(SH):
            dve_names += [("mid", u), ("hid", u)]
        dve_names += DVE_ROUTE[3:]
        dve_names += [("hid", u) for u in range(SH, SH + EX)]
        dve_names += ["y0", "y1"]
        dve_order = Order(dve_names)

        block = ctx.enter_context(nc.Block())

        @block.sync
        def _(sp):
            for t, name in first_loads:
                sp.dma_start(t[:], a[name]).then_inc(s_ld, 16)
            for l in range(2):
                sp.wait_ge(s_set, NSET)
                sp.dma_start(w_b[l][0:1, :, U:NGATE * U], a[f"b_x{l}"]).then_inc(s_ld, 16)
                sp.dma_start(w_b[l][1:2, :, 0:3 * U], a[f"b_h{l}"]).then_inc(s_ld, 16)
            for t, name in late_loads:
                sp.dma_start(t[:], a[name]).then_inc(s_ld2, 16)
            sp_slots(sp, 0, BODY)
            with sp.Fori(1, NBODY):
                sp_slots(sp, BODY, BODY)
            with sp.Fori(0, NTB) as k:
                for i, (c, n) in enumerate(((c_pe, pe_order), (c_act, act_order), (c_dve, dve_order))):
                    sp.wait_ge(c, len(n.value))
                sp.dma_start(out[:, :, bass.ds(k * TB, TB)], y[:]).then_inc(c_out, 16)
                sp.wait_ge(c_out, 16)
                sp.sem_clear(range(c_pe.num, c_pe.num + 4))
                sp.sem_inc(c_go, 1)

        @block.tensor
        def _(pe):
            pe.wait_ge(s_ld, 16 * (len(first_loads) + 4))
            pe.wait_ge(s_set, NSET)
            for i in range(NTB * KT):
                nb, m = divmod(i, KT)
                if i >= 4:
                    pe.wait_ge(s_mix, B * (i - 3))
                for kt in range(KT):
                    mm = pe.matmul(banks[4 + i % 4][:], w_in[:, kt, m * P:(m + 1) * P], x_t[:, kt, nb * TB:(nb + 1) * TB],
                                   start=(kt == 0), stop=(kt == KT - 1))
                mm.then_inc(s_mps, 1)
            pe.wait_ge(s_stg, 1)
            for piece in range(3):
                project(pe, 0, 0, piece, s_x0 if piece == 2 else None)
            pe_slots(pe, 0, BODY)
            with pe.Fori(1, NBODY):
                pe_slots(pe, BODY, BODY)
            pe_slots(pe, T, LAG)

            pe.wait_ge(s_ld2, 16 * len(late_loads))
            pe.wait_ge(s_pick, 1)
            pe.wait_ge(s_hist, 1)
            for m in range(KT):
                for kt in range(KT):
                    pe.matmul(banks[4][:, B * m:B * m + B], w_gate[:, kt, m * P:(m + 1) * P], cond[:, kt, :],
                              start=(kt == 0), stop=(kt == KT - 1))
            for kt in range(KT):
                mm = pe.matmul(banks[5][0:E, 0:B], w_r[:, KT + kt, :], cond[:, kt, :], start=(kt == 0), stop=(kt == KT - 1))
            mm.then_inc(s_mps, 1)
            with pe.Fori(0, NTB) as k:
                pe.wait_ge(c_dve, dve_order.at("gated"))
                for m in range(KT):
                    for kt in range(KT):
                        mm = pe.matmul(H_BANKS[m][:], w_out[:, kt, m * P:(m + 1) * P], gated[:, kt, :],
                                       start=(kt == 0), stop=(kt == KT - 1))
                    mm.then_inc(c_pe, 1)
                pe.wait_ge(c_dve, dve_order.at("x21"))
                for kt in range(KT):
                    mm = pe.matmul(C_BANKS[0][0:E, :], w_r[:, kt, :], x2[:, kt, :], start=(kt == 0), stop=(kt == KT - 1))
                mm.then_inc(c_pe, 1)

                def up(u):
                    kind, i = UNITS[u]
                    if kind == "s":
                        if u >= 2:
                            pe.wait_ge(c_dve, dve_order.at(("hid", u - 2)))
                        for w, bank in ((w_1, H_BANKS[2 * (u % 2)]), (w_3, H_BANKS[2 * (u % 2) + 1])):
                            for kt in range(KT):
                                mm = pe.matmul(bank[:], w[:, kt, i * P:(i + 1) * P], x2[:, kt, :],
                                               start=(kt == 0), stop=(kt == KT - 1))
                    else:
                        e, m = divmod(i, KT)
                        if i == 0:
                            pe.wait_ge(c_dve, dve_order.at("comb_t"))
                        if i < 4:
                            pe.wait_ge(c_dve, dve_order.at(("hid", SH - 1)))
                        else:
                            pe.wait_ge(c_dve, dve_order.at(("hid", u - 3)))
                        if m == 0:
                            mm = pe.matmul(C_BANKS[e % 2][:], pick[:, e, :], comb_t[:], start=True, stop=True)
                        for kt in range(KT):
                            mm = pe.matmul(H_BANKS[i % 4][:], w_1e[:, e, kt, m * P:(m + 1) * P], x2[:, kt, :],
                                           start=(kt == 0), stop=(kt == KT - 1))
                    mm.then_inc(c_pe, 1)

                def down(u):
                    kind, i = UNITS[u]
                    pe.wait_ge(c_dve, dve_order.at(("hid", u)))
                    w = w_2[:, i, :] if kind == "s" else w_2e[:, i // KT, i % KT, :]
                    for m in range(KT):
                        mm = pe.matmul(ACC[m][:], w[:, m * P:(m + 1) * P], hid[u % 3][:],
                                       start=(u == 0), stop=(u == SH + EX - 1))
                    mm.then_inc(c_pe, 1)

                for u in range(SH + EX):
                    up(u)
                    if u >= 2:
                        down(u - 2)
                down(SH + EX - 2)
                down(SH + EX - 1)
                pe.wait_ge(c_go, k + 1)

        @block.vector
        def _(v):
            v.memset(ones[:], 1.0).then_inc(s_set, 1)
            v.memset(mixed[:, :, T * B:], 0.0).then_inc(s_set, 1)
            v.memset(pick[:], 0.0).then_inc(s_set, 1)
            v.memset(scores[:], 0.0).then_inc(s_set, 1)
            v.memset(comb[:], 0.0).then_inc(s_set, 1)
            for l in range(2):
                v.memset(w_b[l][:], 0.0).then_inc(s_set, 1)
                v.memset(slots[l][:], 0.0).then_inc(s_set, 1)
                v.memset(f_r[l][:], 0.0).then_inc(s_set, 1)
                v.memset(f_z[l][:], 0.0).then_inc(s_set, 1)
                v.memset(t_h[l][:], 0.0).then_inc(s_set, 1)
            v.wait_ge(s_ld, 16 * (len(first_loads) + 4))
            for b in range(B):
                last = v.tensor_tensor(in_bias[:, :, b], b_in[:], cond[:, :, b], ALU.add)
            last.then_inc(s_bias, 1)
            v.wait_ge(s_x0, 1)
            turn_xn(v, 0, 0)
            dve_slots(v, 0, BODY)
            with v.Fori(1, NBODY):
                dve_slots(v, BODY, BODY)
            dve_slots(v, T, LAG)
            dve_h(v, 1, T - 1)

            v.wait_ge(s_mix, B * NTB * KT + KT + 1)
            v.tensor_scalar(gate1[:], gsig[:], 1.0, None, ALU.add).then_inc(s_tail, 1)
            for e in range(E):
                for o in range(E):
                    last = v.memset(lower[:, e, o:o + 1], 1.0 if o < e else 0.0)
            last.then_inc(s_tail, 1)
            v.wait_ge(s_tail, 2)
            v.wait_ge(s_hist, 1)

            def put(ins):
                return ins.then_inc(c_dve, 1)

            def after(name):
                v.wait_ge(c_dve, dve_order.at(name))

            with v.Fori(0, NTB) as k:
                here = hist[:, :, bass.ds(k * TB + ROWS, TB)].rearrange("p k (t b) -> p k t b", b=B)
                for b in range(B):
                    for kt in range(KT):
                        last = v.tensor_scalar(gated[:, kt, b::B], here[:, kt, :, b], gate1[:, kt, b:b + 1], None, ALU.mult)
                put(last)
                for m in range(KT):
                    v.wait_ge(c_pe, pe_order.at(f"out{m}"))
                    put(v.scalar_tensor_tensor(x2[:, m, :], H_BANKS[m][:], b_out[:, m:m + 1],
                                               x_t[:, m, bass.ds(k * TB, TB)], ALU.add, ALU.add))

                def hidden(u):
                    kind, i = UNITS[u]
                    v.wait_ge(c_act, act_order.at(("act", u)))
                    if u >= 3:
                        v.wait_ge(c_pe, pe_order.at(("down", u - 3)))
                    if kind == "s":
                        one, two = H_BANKS[2 * (u % 2)], H_BANKS[2 * (u % 2) + 1]
                        put(v.tensor_tensor(mid[u % 2][:], act_t[u % 2][:], one[:], ALU.mult))
                    else:
                        put(v.tensor_tensor(hid[u % 3][:], act_t[u % 2][:], C_BANKS[i // KT % 2][:], ALU.mult))
                        return
                    after(("mid", u))
                    put(v.tensor_tensor(hid[u % 3][:], mid[u % 2][:], two[:], ALU.mult))

                for u in range(SH):
                    hidden(u)
                v.wait_ge(c_act, act_order.at("score1"))
                put(v.tensor_scalar(scores[0:E, 1, :], scores[0:E, 0, :], b_r[:, 0:1], None, ALU.add))
                put(v.transpose(by_tok[:, 0].rearrange("p n e -> p (n e)"), scores[:, 0, :]))
                after("sel_s")
                put(v.transpose(by_tok[:, 1].rearrange("p n e -> p (n e)"), scores[:, 1, :]))
                after("tok1")
                NT = TB // 32
                mine = by_tok[:, 1, :, 0:E].unsqueeze(3).to_broadcast([32, NT, E, E])
                other = by_tok[:, 1, :, 0:E].unsqueeze(2).to_broadcast([32, NT, E, E])
                put(v.tensor_tensor(gt[:], other, mine, ALU.is_gt))
                put(v.tensor_tensor(ge[:], other, mine, ALU.is_ge))
                after("ge")
                put(v.tensor_tensor(ge[:], ge[:], gt[:], ALU.subtract))
                after("d")
                put(v.tensor_tensor(ge[:], ge[:], lower[:].unsqueeze(1).to_broadcast([32, NT, E, E]), ALU.mult))
                after("dl")
                put(v.tensor_tensor(gt[:], gt[:], ge[:], ALU.add))
                after("rk")
                put(v.tensor_reduce(rank[:], gt[:], AX.X, ALU.add))
                after("rank")
                put(v.tensor_scalar(mask[:], rank[:], 1.5, None, ALU.is_lt))
                after("mask")
                put(v.tensor_tensor(sel[:], mask[:], by_tok[:, 0, :, 0:E], ALU.mult))
                after("sel")
                put(v.tensor_reduce(denom[:], sel[:], AX.X, ALU.add))
                after("denom")
                put(v.tensor_scalar(big[:], denom[:], 1e-9, None, ALU.is_gt))
                put(v.tensor_scalar(recip[:], denom[:], 1e-9, None, ALU.add))
                after("dplus")
                put(v.reciprocal(recip[:], recip[:]))
                after("recip")
                put(v.tensor_tensor(recip[:], recip[:], big[:], ALU.mult))
                put(v.tensor_scalar(tie[:], big[:], -0.5, 0.5, ALU.mult, ALU.add))
                after("tie")
                put(v.tensor_tensor(sel[:], sel[:], recip[:].unsqueeze(2).to_broadcast([32, NT, E]), ALU.mult))
                put(v.tensor_tensor(mask[:], mask[:], tie[:].unsqueeze(2).to_broadcast([32, NT, E]), ALU.mult))
                after("w_tie")
                put(v.tensor_tensor(comb[:, :, 0:E], sel[:], mask[:], ALU.add))
                after("comb")
                put(v.transpose(comb_t[:], comb[:].rearrange("p n e -> p (n e)")))
                for u in range(SH, SH + EX):
                    hidden(u)
                v.wait_ge(c_pe, pe_order.at(("down", SH + EX - 1)))
                for m in range(KT):
                    put(v.scalar_tensor_tensor(y[:, m, :], ACC[m][:], 1.0 / 3.0, x2[:, m, :], ALU.mult, ALU.add))
                v.wait_ge(c_go, k + 1)

        @block.scalar
        def _(act):
            act.wait_ge(s_bias, 1)
            for i in range(NTB * KT):
                nb, m = divmod(i, KT)
                act.wait_ge(s_mps, i + 1)
                for b in range(B):
                    act.activation(mixed[:, m, nb * TB + b:(nb + 1) * TB:B], banks[4 + i % 4][:, b::B], ACT.Tanh,
                                   bias=in_bias[:, m, b:b + 1]).then_inc(s_mix, 1)
            act_slots(act, 0, BODY)
            with act.Fori(1, NBODY):
                act_slots(act, BODY, BODY)
            act_slots(act, T, LAG)

            act.wait_ge(s_mps, NTB * KT + 1)
            for m in range(KT):
                act.activation(gsig[:, m, :], banks[4][:, B * m:B * m + B], ACT.Sigmoid, bias=b_gate[:, m:m + 1])\
                   .then_inc(s_mix, 1)
            act.activation(r_bias[:], banks[5][0:E, 0:B], ACT.Identity).then_inc(s_mix, 1)
            act.wait_ge(s_mix, B * NTB * KT + KT + 1)
            with act.Fori(0, NTB) as k:
                act.wait_ge(c_pe, pe_order.at("route"))
                for b in range(B):
                    act.activation(scores[0:E, 0, b::B], C_BANKS[0][0:E, b::B], ACT.Sigmoid, bias=r_bias[:, b:b + 1])\
                       .then_inc(c_act, 1)
                for u in range(SH + EX):
                    kind, i = UNITS[u]
                    act.wait_ge(c_pe, pe_order.at(("up", u)))
                    if u >= 2:
                        act.wait_ge(c_dve, dve_order.at(("mid" if u - 2 < SH else "hid", u - 2)))
                    if kind == "s":
                        act.activation(act_t[u % 2][:], H_BANKS[2 * (u % 2)][:], ACT.Sigmoid).then_inc(c_act, 1)
                    else:
                        act.activation(act_t[u % 2][:], H_BANKS[i % 4][:], ACT.Gelu).then_inc(c_act, 1)
                act.wait_ge(c_go, k + 1)

        @block.gpsimd
        def _(pool):
            pool.wait_ge(s_set, NSET)
            pool.affine_select(out=pick[:], in_=pick[:], compare_op=ALU.not_equal, fill=1.0, base=0,
                               pattern=[[-1, E], [0, P]], channel_multiplier=1).then_inc(s_pick, 1)
            pool.wait_ge(s_mix, B * KT)
            pool.tensor_copy(stage[0][:], mixed[:, :, 0:ROWS]).then_inc(s_stg, 1)
            pool.wait_ge(s_x0, 1)
            pool.wait_ge(s_mix, B * NTB * KT)
            pool_slots(pool, 0, BODY, lambda c: bass.ds(c * ROWS, ROWS))
            with pool.Fori(1, NBODY) as k:
                pool_slots(pool, BODY, BODY, lambda c: bass.ds(k * (BODY * B) + (c * ROWS - BODY * B), ROWS))
            pool_slots(pool, T, LAG, lambda c: bass.ds(c * ROWS, ROWS))
            pool.wait_ge(sets[1][1]["dve"], dve_at(CH - 1, "h"))
            read_out(pool, 1, hist[:, :, T * B:], s_hist)


def _gate_columns(w, order):
    import numpy as np
    g = w.reshape((3, NQ, U) + w.shape[1:])
    g = np.stack([g[i] for i in order], axis=1)
    return np.moveaxis(g.reshape((NQ, 3 * U) + w.shape[1:]), (0, 1), (-2, -1))


def _state_rows(w):
    return w.reshape((NQ, UB, 32) + w.shape[1:]).swapaxes(1, 2).reshape((P, KT) + w.shape[1:])


def _rows(w):
    return w.reshape((-1, P) + w.shape[1:]).swapaxes(0, 1)


def kernel(**inputs):
    import numpy as np
    import concourse.bacc as bacc
    from concourse.bass_utils import run_bass_kernel_spmd

    i = {k: np.asarray(v) for k, v in inputs.items()}
    R, Z, N = 0, 1, 2
    tok = lambda v: v.transpose(2, 1, 0).reshape(D, T * B)
    arrays = {
        "x_t": _rows(tok(i["x"])), "cond": _rows(i["cond_1024"].T),
        "w_in": _rows(i["L0_cond_W_in"].T), "b_in": _rows(i["L0_cond_b_in"]),
        "w_out": _state_rows(i["L0_cond_W_out"].T), "b_out": _rows(i["L0_cond_b_out"]),
        "w_gate": _rows(_state_rows(i["L0_cond_W_gate"]).swapaxes(0, 1).reshape(D, D).T),
        "b_gate": _state_rows(i["L0_cond_b_gate"]),
        "w_r": _rows(i["L1_cond_router_W"]), "b_r": i["L1_cond_router_bias"].reshape(E, 1),
        "w_1": _rows(i["L1_cond_w1"]), "w_3": _rows(i["L1_cond_w3"]), "w_2": _rows(i["L1_cond_w2"]),
        "w_1e": i["L1_cond_W1e"].reshape(E, KT, P, HE).transpose(2, 0, 1, 3),
        "w_2e": i["L1_cond_W2e"].reshape(E, KT, P, D).transpose(2, 0, 1, 3),
    }
    for l in range(2):
        rows = _state_rows if l else _rows
        arrays[f"w_x{l}"] = rows(_gate_columns(i[f"L0_cond_Wih{l}"], (Z, R, N)))
        arrays[f"w_h{l}"] = _state_rows(_gate_columns(i[f"L0_cond_Whh{l}"], (N, Z, R)))
        arrays[f"b_x{l}"] = _gate_columns(i[f"L0_cond_bih{l}"], (Z, R, N))[None]
        arrays[f"b_h{l}"] = _gate_columns(i[f"L0_cond_bhh{l}"], (N, Z, R))[None]
    arrays = {k: np.ascontiguousarray(v) for k, v in arrays.items()}

    nc = bacc.Bacc("TRN2", target_bir_lowering=False, num_devices=1)
    a = {k: nc.dram_tensor(f"in_{k}", v.shape, F32, kind="ExternalInput").ap() for k, v in arrays.items()}
    out = nc.dram_tensor("out_y", (P, KT, T * B), F32, kind="ExternalOutput").ap()
    gru_moe_kernel(nc, a, out)
    r = run_bass_kernel_spmd(nc, [{f"in_{k}": v for k, v in arrays.items()}], core_ids=[0])
    y = r.results[0]["out_y"]
    return y.reshape(P, KT, T, B).transpose(3, 2, 1, 0).reshape(B, T, D)
```

```python
from contextlib import ExitStack

import concourse.bass as bass
from concourse import mybir
from concourse.alu_op_type import AluOpType as ALU

ACT = mybir.ActivationFunctionType
AX = mybir.AxisListType
F32 = mybir.dt.float32

P = 128
B, T, D = 2, 1024, 256
KT = D // P
NQ = 4
U = D // NQ
UB = U // 32
NGATE = 4
CH = 16
ROWS = CH * B
BODY = 4 * CH
LAG = CH + 4
ELT = 3
PITCH = ROWS * UB * ELT
OWN = B * UB * ELT
DIAG = PITCH + OWN
HS, E, HE = 512, 8, 256
TG = BODY * B
MLAG = BODY + LAG + 4
SH = HS // P
UNITS = [("s", i) for i in range(SH)] + [("e", i) for i in range(E)]
TSTEP = 2 * BODY
HALF = TSTEP // 2

DVE_STEP = ("r_t", "hnz_t", "pre_n", "omz2", "zh2", "h")
ACT_STEP = ("r", "z", "n")


def dve_at(j, what):
    return len(DVE_STEP) * j + DVE_STEP.index(what) + 1


def act_at(j, what):
    return len(ACT_STEP) * j + ACT_STEP.index(what) + 1


def projection_pieces():
    return {6: (0, 0), 8: (0, 1), 10: (0, 2), 0: (1, 0), 1: (1, 1), 2: (1, 2)}


class Mixture:

    def __init__(self):
        self.ops = {k: [] for k in ("pe", "act", "dve", "pool")}
        self.when, self.value, self.engine = {}, {}, {}

    def add(self, engine, name, waits, issue, beside=False):
        pieces = projection_pieces()
        busy = lambda h: engine == "pe" and h % 2 == 0 and (h // 2 + MLAG) % CH in pieces
        last = self.ops[engine][-1][0] if self.ops[engine] else -1
        h = max([self.when[w] + 1 for w in waits] + [last + (0 if beside else 1)])
        while busy(h):
            h += 1
        assert h < TSTEP, (name, h)
        done_before = [n for n, e in self.engine.items() if e == engine and self.when[n] // HALF == h // HALF]
        self.when[name], self.engine[name], self.value[name] = h, engine, len(done_before) + 1
        self.ops[engine].append((h, name, waits, issue))

    def half(self, name):
        return self.when[name] // HALF

    def total(self, engine, half):
        return sum(1 for n, e in self.engine.items() if e == engine and self.half(n) == half)

    def past_half(self, engine, half):
        mine = [o for o in self.ops[engine] if o[0] // HALF == half]
        late = [k for k, o in enumerate(mine) if any(self.half(w) != half for w in o[2])]
        return max(late, default=0) + 1

    def past_slot(self, half):
        at = [[o[0] for o in self.ops[k] if o[0] // HALF == half][self.past_half(k, half) - 1] for k in ("pe", "act", "dve")]
        return max(at) // 2


def gru_moe_kernel(nc, a, out):
    with ExitStack() as ctx:
        def sb(name, *shape):
            return ctx.enter_context(nc.sbuf_tensor(name, list(shape), F32))

        def sem(name):
            return ctx.enter_context(nc.semaphore(name))

        w_in = sb("w_in", P, KT, D)
        w_x = [sb(f"w_x{l}", P, KT, NQ, 3 * U) for l in range(2)]
        w_h = [sb(f"w_h{l}", P, KT, NQ, 3 * U) for l in range(2)]
        w_b = [sb(f"w_b{l}", P, NQ, NGATE * U) for l in range(2)]
        w_out = sb("w_out", P, KT, D)
        w_gate = sb("w_gate", P, KT, D)
        w_r = sb("w_r", P, 2 * KT, E)
        w_1 = sb("w_1", P, KT, HS)
        w_3 = sb("w_3", P, KT, HS)
        w_2 = sb("w_2", P, SH, D)
        w_1e = sb("w_1e", P, E, KT, HE)
        w_2e = sb("w_2e", P, E, KT, D)
        b_in = sb("b_in", P, KT)
        b_out = sb("b_out", P, KT)
        b_gate = sb("b_gate", P, KT)
        b_r = sb("b_r", E, 1)
        cond = sb("cond", P, KT, B)
        ones = sb("ones", P, ROWS)
        x_t = sb("x_t", P, KT, T * B)
        mixed = sb("mixed", P, KT, T * B + ROWS)
        hist = sb("hist", P, KT, ROWS + T * B)
        in_bias = sb("in_bias", P, KT, B)
        gate_th = sb("gate_th", P, KT, B)
        gate1 = sb("gate1", P, KT, B)
        b_gate_half = sb("b_gate_half", P, KT)
        r_bias = sb("r_bias", E, B)
        stage = [sb(f"stage{l}", P, KT, ROWS) for l in range(2)]
        slots = [sb(f"slots{l}", P, CH * DIAG) for l in range(2)]
        r_pre = [sb(f"r_pre{l}", P, ROWS, UB) for l in range(2)]
        r_first = [sb(f"r_first{l}", P, 2, ROWS, UB, ELT) for l in range(2)]
        r_second = [[sb(f"r_second{l}_{p}", P, ROWS, UB, ELT) for p in range(2)] for l in range(2)]
        n_scan = [sb(f"n_scan{l}", P, B * UB, ELT) for l in range(2)]
        h_first = [sb(f"h_first{l}", P, B * UB, ELT) for l in range(2)]
        h_second = [sb(f"h_second{l}", P, B * UB, ELT) for l in range(2)]
        z_th = [sb(f"z_th{l}", P, B * UB) for l in range(2)]
        gated = sb("gated", P, KT, TG)
        x2 = sb("x2", P, KT, TG)
        y = sb("y", P, KT, TG)
        NB = TG // 32
        score_th = sb("score_th", E, TG)
        scores = sb("scores", 32, 2, TG)
        by_tok = sb("by_tok", 32, 2, NB, 32)
        gt = sb("gt", 32, NB, E, E)
        ge = sb("ge", 32, NB, E, E)
        lower = sb("lower", 32, E, E)
        rank = sb("rank", 32, NB, E)
        mask = sb("mask", 32, NB, E)
        sel = sb("sel", 32, NB, E)
        denom = sb("denom", 32, NB)
        big = sb("big", 32, NB)
        recip = sb("recip", 32, NB)
        tie = sb("tie", 32, NB)
        comb = sb("comb", 32, NB, 32)
        comb_t = sb("comb_t", 32, TG)
        pick = sb("pick", 32, E, P)
        c_all = sb("c_all", P, E, TG)
        act_t = [sb(f"act_t{i}", P, KT, TG) for i in range(2)]
        mid = sb("mid", P, TG)
        hid = [sb(f"hid{i}", P, KT, TG) for i in range(2)]

        banks = [ctx.enter_context(nc.psum_tensor(f"bank{i}", [P, 512], F32)) for i in range(8)]
        gates = [[banks[2 * l + p] for p in range(2)] for l in range(2)]
        acc = banks[4][:, 0:KT * TG].rearrange("p (m n) -> p m n", m=KT)
        ups = [banks[5 + i][:, 0:2 * TG].rearrange("p (m n) -> p m n", m=2) for i in range(2)]
        misc = banks[7][:, :].rearrange("p (m n) -> p m n", n=TG)

        s_ld = sem("s_ld")
        s_xld = sem("s_xld")
        s_bld = sem("s_bld")
        s_mld = sem("s_mld")
        s_set = sem("s_set")
        s_bias = sem("s_bias")
        s_pick = sem("s_pick")
        s_mps = sem("s_mps")
        s_cps = sem("s_cps")
        s_mix = sem("s_mix")
        s_gate = sem("s_gate")
        s_stg = sem("s_stg")
        s_x0 = sem("s_x0")
        s_hist = sem("s_hist")
        KINDS = ("pe", "dve", "act", "pool", "x", "xn", "go")
        sets = [[{k: sem(f"s_{k}{l}_{p}") for k in KINDS} for p in range(2)] for l in range(2)]
        m_sets = [{k: sem(f"m_{k}_{p}") for k in ("pe", "dve", "act", "pool", "out", "go")} for p in range(2)]

        def numbers(semaphores):
            nums = [s.num for s in semaphores.values()]
            assert nums == list(range(nums[0], nums[0] + len(nums)))
            return range(nums[0], nums[0] + len(nums))

        first_loads = [(w_in, "w_in"), (b_in, "b_in"), (cond, "cond"), (w_gate, "w_gate"), (b_gate, "b_gate"), (w_r, "w_r")]
        gru_loads = [(w_x[0], "w_x0"), (w_h[0], "w_h0"), (w_x[1], "w_x1"), (w_h[1], "w_h1")]
        late_loads = [(w_out, "w_out"), (w_1, "w_1"), (w_3, "w_3"), (w_2, "w_2"), (w_1e, "w_1e"), (w_2e, "w_2e"),
                      (b_out, "b_out"), (b_r, "b_r")]
        TB = 512
        NTB = B * T // TB

        def triples(tile):
            return tile[:].rearrange("p c e -> p (c e)")

        def own_rows(tile, j):
            return tile[:, B * j:B * j + B].rearrange("p i b e -> p (i b) e")

        def slot_state(l, j):
            return slots[l][:, j * DIAG:j * DIAG + OWN].rearrange("p (c e) -> p c e", e=ELT)

        def slot_tile(l, j, kt):
            at = j * PITCH + kt * ELT + ELT - 1
            step = UB * ELT
            return slots[l][:, at:at + (ROWS - 1) * step + 1:step]

        def schedule(s0, n):
            for s in range(s0, s0 + n):
                yield s, (s if s < T else None), (s - LAG if 0 <= s - LAG < T else None)

        def project(pe, l, p, piece, last=None):
            ps = gates[l][p]
            for g in range(NQ):
                rows = ps[32 * g:32 * g + 32, :]
                if piece == 0:
                    mm = pe.matmul(rows[:, 0:NGATE * U], ones[:, :], w_b[l][:, g, :], start=True, stop=False,
                                   tile_position=(0, 32 * g), skip_group_check=True)
                else:
                    mm = pe.matmul(rows[:, U:NGATE * U], stage[l][:, piece - 1, :], w_x[l][:, piece - 1, g, :],
                                   start=False, stop=False, tile_position=(0, 32 * g), skip_group_check=True)
            if last is not None:
                mm.then_inc(last, 1)

        def recur(pe, l, t):
            p, j = t // CH % 2, t % CH
            s = sets[l][p]
            if j:
                pe.wait_ge(s["dve"], dve_at(j - 1, "h"))
            elif t >= CH:
                pe.wait_ge(sets[l][1 - p]["dve"], dve_at(CH - 1, "h"))
            if j == 0:
                pe.wait_ge(sets[l][1 - p]["xn"], 1)
            if j == CH - 1 and t < T - 1:
                pe.wait_ge(s["go"], 1)
            for kt in range(KT):
                for g in range(NQ):
                    mm = pe.matmul(gates[l][p][32 * g:32 * g + 32, 0:3 * U], slot_tile(l, j, kt), w_h[l][:, kt, g, :],
                                   start=False, stop=False, tile_position=(0, 32 * g), skip_group_check=True)
            mm.then_inc(s["pe"], 1)

        def pe_slots(pe, s0, n, base):
            for s, t0, t1 in schedule(s0, n):
                c, j = divmod(s, CH)
                p = c % 2
                if t0 is not None:
                    recur(pe, 0, t0)
                l, piece = projection_pieces().get(j, (None, None))
                if l == 1 and CH <= s < T + CH:
                    if piece == 0:
                        pe.wait_ge(sets[0][p]["pool"], 1)
                    project(pe, 1, 1 - p, piece, sets[1][p]["x"] if piece == 2 else None)
                if l == 0 and t0 is not None:
                    if piece == 0:
                        pe.wait_ge(sets[0][p]["pool"], 2)
                    project(pe, 0, 1 - p, piece, sets[0][p]["x"] if piece == 2 else None)
                mixture_at(pe, "pe", s, 0, base)
                if t1 is not None:
                    recur(pe, 1, t1)
                mixture_at(pe, "pe", s, 1, base)

        def blocks(ap):
            return ap.rearrange("p (b i) -> p b i", i=32)

        def turn_xn(v, l, p):
            v.transpose(r_second[l][p][:, :, :, ELT - 1].rearrange("p i b -> p b i"),
                        blocks(gates[l][p][:, 3 * U:4 * U])).then_inc(sets[l][1 - p]["xn"], 1)

        def dve_step(v, l, t):
            p, j = t // CH % 2, t % CH
            s = sets[l][p]
            v.wait_ge(s["pe"], j + 1)
            if j == 0:
                v.wait_ge(sets[l][1 - p]["xn"], 1)
            if j == CH - 1 and t < T - 1:
                v.wait_ge(s["go"], 1)
            v.transpose(r_pre[l][:].rearrange("p i b -> p b i"), blocks(gates[l][p][:, 2 * U:3 * U])).then_inc(s["dve"], 1)
            v.transpose(r_first[l][:].rearrange("p g i b e -> p e g b i")[:, ELT - 1],
                        gates[l][p][:, 0:2 * U].rearrange("p (g b i) -> p g b i", g=2, i=32)).then_inc(s["dve"], 1)
            v.wait_ge(s["act"], act_at(j, "r"))
            v.wait_ge(s["dve"], dve_at(j, "hnz_t"))
            v.tensor_tensor_scan(triples(n_scan[l]), own_rows(r_first[l][:, 0], j).rearrange("p c e -> p (c e)"),
                                 own_rows(r_second[l][p], j).rearrange("p c e -> p (c e)"), 0.0, ALU.mult, ALU.add)\
                .then_inc(s["dve"], 1)
            v.wait_ge(s["act"], act_at(j, "z"))
            v.tensor_scalar(h_first[l][:, :, 1], z_th[l][:], -1.0, 1.0, ALU.mult, ALU.add).then_inc(s["dve"], 1)
            v.scalar_tensor_tensor(h_second[l][:, :, 1], z_th[l][:], 1.0, slot_state(l, j)[:, :, ELT - 1], ALU.add, ALU.mult)\
                .then_inc(s["dve"], 1)

        def dve_h(v, l, t):
            p, j = t // CH % 2, t % CH
            s = sets[l][p]
            v.wait_ge(s["act"], act_at(j, "n"))
            v.wait_ge(s["dve"], dve_at(j, "zh2"))
            if j == 0:
                v.wait_ge(s["pool"], 1)
            v.tensor_tensor_scan(slot_state(l, (j + 1) % CH).rearrange("p c e -> p (c e)"), triples(h_first[l]),
                                 triples(h_second[l]), 0.0, ALU.mult, ALU.add).then_inc(s["dve"], 1)

        def dve_slots(v, s0, n, base):
            for s, t0, t1 in schedule(s0, n):
                c, j = divmod(s, CH)
                p = c % 2
                if 0 <= s - 1 - LAG < T:
                    dve_h(v, 1, s - 1 - LAG)
                if t0 is not None:
                    dve_step(v, 0, t0)
                    if j == 12:
                        v.wait_ge(sets[0][p]["x"], 1)
                        turn_xn(v, 0, 1 - p)
                if CH <= s < T + CH and j == 3:
                    v.wait_ge(sets[1][p]["x"], 1)
                    turn_xn(v, 1, 1 - p)
                mixture_at(v, "dve", s, 0, base)
                if t0 is not None:
                    dve_h(v, 0, t0)
                if t1 is not None:
                    dve_step(v, 1, t1)
                mixture_at(v, "dve", s, 1, base)

        def act_step(act, l, t):
            p, j = t // CH % 2, t % CH
            s = sets[l][p]
            act.wait_ge(s["dve"], dve_at(j, "r_t"))
            if j == CH - 1 and t < T - 1:
                act.wait_ge(s["go"], 1)
            own = r_pre[l][:, B * j:B * j + B, :].rearrange("p i b -> p (i b)")
            act.activation(own_rows(r_second[l][p], j)[:, :, 0], own, ACT.Tanh, scale=0.5).then_inc(s["act"], 1)
            act.wait_ge(s["dve"], dve_at(j, "hnz_t"))
            act.activation(z_th[l][:], own_rows(r_first[l][:, 1], j)[:, :, ELT - 1], ACT.Tanh, scale=0.5).then_inc(s["act"], 1)
            act.wait_ge(s["dve"], dve_at(j, "pre_n"))
            act.activation(h_second[l][:, :, 0], n_scan[l][:, :, ELT - 1], ACT.Tanh).then_inc(s["act"], 1)

        def act_slots(act, s0, n, base):
            for s, t0, t1 in schedule(s0, n):
                if t0 is not None:
                    act_step(act, 0, t0)
                mixture_at(act, "act", s, 0, base)
                if t1 is not None:
                    act_step(act, 1, t1)
                mixture_at(act, "act", s, 1, base)

        def read_out(pool, l, dst, done):
            by = slots[l][:].rearrange("p (j r) -> p j r", r=DIAG)
            view = dst.rearrange("p k (j b) -> p k j b", b=B)
            for kt in range(KT):
                own = by[:, :, 0:OWN].rearrange("p j (b k e) -> p j b k e", b=B, e=ELT)[:, :, :, kt, ELT - 1]
                pool.tensor_copy(view[:, kt, 0:CH - 1], own[:, 1:CH])
                last = pool.tensor_copy(view[:, kt, CH - 1], own[:, 0])
            last.then_inc(done, 1)

        def pool_slots(pool, s0, n, base):
            for s, t0, t1 in schedule(s0, n):
                c, j = divmod(s, CH)
                p = c % 2
                if j == 0 and s <= T:
                    if s >= CH:
                        pool.wait_ge(sets[0][1 - p]["go"], 1)
                        pool.wait_ge(sets[0][1 - p]["dve"], dve_at(CH - 1, "h"))
                    read_out(pool, 0, stage[1][:], sets[0][p]["pool"])
                    if t0 is not None:
                        pool.tensor_copy(stage[0][:], mixed[:, :, bass.ds(base + (c + 1) * ROWS, ROWS)])\
                            .then_inc(sets[0][p]["pool"], 1)
                if t1 is not None and t1 % CH == 0:
                    cb = t1 // CH
                    pb = cb % 2
                    if t1 >= CH:
                        pool.wait_ge(sets[1][1 - pb]["go"], 1)
                        pool.wait_ge(sets[1][1 - pb]["dve"], dve_at(CH - 1, "h"))
                    read_out(pool, 1, hist[:, :, bass.ds(base + cb * ROWS, ROWS)], sets[1][pb]["pool"])
                if s == T + LAG:
                    pool.wait_ge(sets[1][1]["dve"], dve_at(CH - 1, "h"))
                    read_out(pool, 1, hist[:, :, T * B:], s_hist)
                mixture_at(pool, "pool", s, 0, base)
                mixture_at(pool, "pool", s, 1, base)

        def sp_slots(sp, s0, n, base):
            for s, t0, t1 in schedule(s0, n):
                for l, t in ((0, t0), (1, t1)):
                    if t is not None and t % CH == 0:
                        p = t // CH % 2
                        now = sets[l][p]
                        for k in ("pe", "dve", "act"):
                            sp.wait_ge(now[k], 1)
                        sp.wait_ge(now["pool"], 2 - l)
                        sp.sem_clear(numbers(sets[l][1 - p]))
                        sp.sem_inc(now["go"], 1)
                m = s - MLAG
                if not 0 <= m < T:
                    continue
                if m % BODY == mix.when["y1"] // 2:
                    sp.wait_ge(m_sets[1]["dve"], mix.value["y1"])
                    sp.dma_start(out[:, :, bass.ds(base + m // BODY * TG, TG)], y[:]).then_inc(m_sets[1]["out"], 16)
                    sp.wait_ge(m_sets[1]["out"], 16)
                for half in range(2):
                    if m % BODY != mix.past_slot(half):
                        continue
                    for k in ("pe", "dve", "act"):
                        sp.wait_ge(m_sets[half][k], mix.past_half(k, half))
                    if half == 0:
                        sp.wait_ge(m_sets[half]["pool"], 1)
                    sp.sem_clear(numbers(m_sets[1 - half]))
                    sp.sem_inc(m_sets[half]["go"], 1)

        mix = Mixture()

        def wait_for(eng, name):
            eng.wait_ge(m_sets[mix.half(name)][mix.engine[name]], mix.value[name])

        def mixture_at(eng, engine, s, part, base):
            m = s - MLAG
            if not 0 <= m < T:
                return
            group, h = m // BODY, m % BODY * 2 + part
            for at, name, waits, issue in mix.ops[engine]:
                if at != h:
                    continue
                for w in waits:
                    wait_for(eng, w)
                half = h // HALF
                if name == "out00" and group > 0:
                    eng.wait_ge(m_sets[1]["dve"], mix.value["y1"])
                if name == "gated":
                    eng.wait_ge(*((sets[1][0]["pool"], 1) if group < T // BODY - 1 else (s_hist, 1)))
                if mix.value[name] == mix.total(engine, half) and (group, half) != (T // BODY - 1, 1) \
                        and not (engine == "pool"):
                    eng.wait_ge(m_sets[half]["go"], 1)
                issue(eng, base + group * TG).then_inc(m_sets[half][engine], 1)

        def product(ps, w, x, start, stop):
            return lambda pe, col: pe.matmul(ps, w, x, start=start, stop=stop, skip_group_check=True)

        def feature_tile(w, m):
            return w[:, m * P:(m + 1) * P]

        gated4 = gated[:].rearrange("p k (t b) -> p k t b", b=B)
        mix.add("pool", "gated", (), lambda pool, col: pool.tensor_tensor(
            gated4, hist[:, :, bass.ds(col + ROWS, TG)].rearrange("p k (t b) -> p k t b", b=B),
            gate1[:].unsqueeze(2).to_broadcast([P, KT, BODY, B]), ALU.mult))
        for m in range(KT):
            for kt in range(KT):
                mix.add("pe", f"out{m}{kt}", ("gated",) if m == kt == 0 else (),
                        product(misc[:, m], feature_tile(w_out[:, kt], m), gated[:, kt], m == kt == 0, kt == KT - 1), beside=kt > 0)
        for m in range(KT):
            mix.add("dve", f"x2{m}", (f"out{KT - 1}{KT - 1}",), lambda v, col, m=m: v.scalar_tensor_tensor(
                x2[:, m], misc[:, m], b_out[:, m:m + 1], x_t[:, m, bass.ds(col, TG)], ALU.add, ALU.add))
        for kt in range(KT):
            mix.add("pe", f"route{kt}", ("x21",), product(misc[0:E, 0], w_r[:, kt], x2[:, kt], kt == 0, kt == KT - 1), beside=kt > 0)
        for b in range(B):
            mix.add("act", f"score{b}", (f"route{KT - 1}",), lambda act, col, b=b: act.activation(
                score_th[:, b::B], misc[0:E, 0, b::B], ACT.Tanh, bias=r_bias[:, b:b + 1], scale=0.5))

        def up(u):
            kind, i = UNITS[u]
            free = () if u < 2 else (f"hid{u - 2}",)
            for h in range(2):
                for kt in range(KT):
                    if kind == "s":
                        w = feature_tile((w_1, w_3)[h][:, kt], i)
                    else:
                        w = feature_tile(w_1e[:, i, kt], h)
                    mix.add("pe", f"up{u}_{h}{kt}", free if h == kt == 0 else (),
                            product(ups[u % 2][:, h], w, x2[:, kt], h == kt == 0, kt == KT - 1))

        def nonlinear(u):
            kind, i = UNITS[u]
            bank, done = ups[u % 2], f"up{u}_{1}{KT - 1}"
            read = () if u < 2 else (f"hid{u - 2}",)
            if kind == "s":
                mix.add("act", f"act{u}", (done,) + read, lambda act, col: act.activation(
                    act_t[u % 2][:, 0], bank[:, 0], ACT.Tanh, scale=0.5))
                mix.add("dve", f"mid{u}", (f"act{u}",), lambda v, col: v.scalar_tensor_tensor(
                    mid[:], act_t[u % 2][:, 0], 1.0, bank[:, 0], ALU.add, ALU.mult))
                freed = () if u < 2 else (f"down{u - 2}",)
                mix.add("dve", f"hid{u}", (f"mid{u}",) + freed, lambda v, col: v.scalar_tensor_tensor(
                    hid[u % 2][:, 0], mid[:], 0.5, bank[:, 1], ALU.mult, ALU.mult))
            else:
                mix.add("act", f"act{u}", (done,) + read, lambda act, col: act.activation(
                    act_t[u % 2][:], bank[:, :], ACT.Gelu))

        def weigh(u):
            kind, i = UNITS[u]
            if kind == "e":
                mix.add("dve", f"hid{u}", (f"act{u}", f"down{u - 2}") + ((f"gates{i}",) if i < 2 else ()), lambda v, col: v.tensor_tensor(
                    hid[u % 2][:], act_t[u % 2][:], c_all[:, i].unsqueeze(1).to_broadcast([P, KT, TG]), ALU.mult))

        def down(u):
            kind, i = UNITS[u]
            tiles = [w_2[:, i]] if kind == "s" else [w_2e[:, i, kt] for kt in range(KT)]
            for k, w in enumerate(tiles):
                for m in range(KT):
                    last = k == len(tiles) - 1 and m == KT - 1
                    name = f"down{u}" if last else f"down{u}_{k}{m}"
                    mix.add("pe", name, (f"hid{u}",) if k == m == 0 else (),
                            product(acc[:, m], feature_tile(w, m), hid[u % 2][:, k], u == k == m == 0, u == len(UNITS) - 1 and last),
                            beside=kind == "s" and m > 0)

        mine = by_tok[:, 1, :, 0:E].unsqueeze(3).to_broadcast([32, NB, E, E])
        other = by_tok[:, 1, :, 0:E].unsqueeze(2).to_broadcast([32, NB, E, E])
        per_expert = [32, NB, E]
        flat = lambda t: t.rearrange("p n e -> p (n e)")
        ROUTE = [
            ("s", "score1", lambda v, col: v.tensor_scalar(scores[0:E, 0], score_th[:], 0.5, 0.5, ALU.mult, ALU.add)),
            ("s_bias", "s", lambda v, col: v.tensor_scalar(scores[0:E, 1], scores[0:E, 0], b_r[:, 0:1], None, ALU.add)),
            ("tok0", "s", lambda v, col: v.transpose(flat(by_tok[:, 0]), scores[:, 0])),
            ("tok1", "s_bias", lambda v, col: v.transpose(flat(by_tok[:, 1]), scores[:, 1])),
            ("gt", "tok1", lambda v, col: v.tensor_tensor(gt[:], other, mine, ALU.is_gt)),
            ("ge", "tok1", lambda v, col: v.tensor_tensor(ge[:], other, mine, ALU.is_ge)),
            ("equal", "ge", lambda v, col: v.tensor_tensor(ge[:], ge[:], gt[:], ALU.subtract)),
            ("before", "equal", lambda v, col: v.tensor_tensor(
                ge[:], ge[:], lower[:].unsqueeze(1).to_broadcast([32, NB, E, E]), ALU.mult)),
            ("count", "before", lambda v, col: v.tensor_tensor(gt[:], gt[:], ge[:], ALU.add)),
            ("rank", "count", lambda v, col: v.tensor_reduce(rank[:], gt[:], AX.X, ALU.add)),
            ("mask", "rank", lambda v, col: v.tensor_scalar(mask[:], rank[:], 1.5, None, ALU.is_lt)),
            ("sel", "mask", lambda v, col: v.tensor_tensor(sel[:], mask[:], by_tok[:, 0, :, 0:E], ALU.mult)),
            ("denom", "sel", lambda v, col: v.tensor_reduce(denom[:], sel[:], AX.X, ALU.add)),
            ("big", "denom", lambda v, col: v.tensor_scalar(big[:], denom[:], 1e-9, None, ALU.is_gt)),
            ("dplus", "denom", lambda v, col: v.tensor_scalar(denom[:], denom[:], 1e-9, None, ALU.add)),
            ("recip", "dplus", lambda v, col: v.reciprocal(recip[:], denom[:])),
            ("tie", "big", lambda v, col: v.tensor_scalar(tie[:], big[:], -0.5, 0.5, ALU.mult, ALU.add)),
            ("scale", "recip", lambda v, col: v.tensor_tensor(recip[:], recip[:], big[:], ALU.mult)),
            ("w_tie", "tie", lambda v, col: v.tensor_tensor(mask[:], mask[:], tie[:].unsqueeze(2).to_broadcast(per_expert), ALU.mult)),
            ("w_sel", "scale", lambda v, col: v.tensor_tensor(sel[:], sel[:], recip[:].unsqueeze(2).to_broadcast(per_expert), ALU.mult)),
            ("comb", "w_sel", lambda v, col: v.tensor_tensor(comb[:, :, 0:E], sel[:], mask[:], ALU.add)),
            ("comb_t", "comb", lambda v, col: v.transpose(comb_t[:], flat(comb[:]))),
        ]

        def route(n):
            for _ in range(n):
                name, after, issue = ROUTE.pop(0)
                mix.add("dve", name, (after,), issue, beside=name in ("tok0", "dplus", "tie", "w_tie"))

        for u in range(SH):
            up(u)
            if u >= 1:
                nonlinear(u - 1)
            route(3)
            if u >= 2:
                down(u - 2)
        nonlinear(SH - 1)
        route(len(ROUTE))
        down(SH - 2)
        down(SH - 1)
        for q in range(2):
            up(SH + q)
        for q in range(2):
            for i in range(4):
                mix.add("pe", f"spread{q}{i}", (f"gates{q - 1}",) if q and i == 0 else ("comb_t",) if i == 0 else (),
                        product(misc[:, i], pick[:, 4 * q + i], comb_t[:], i == 0, True))
            mix.add("act", f"gates{q}", (f"spread{q}3",), lambda act, col, q=q: act.activation(
                c_all[:, 4 * q:4 * q + 4], misc[:, :], ACT.Identity))
            if q == 0:
                nonlinear(SH)
        for u in range(SH + 2, len(UNITS) + 2):
            weigh(u - 2)
            if u - 1 < len(UNITS):
                nonlinear(u - 1)
            down(u - 2)
            if u < len(UNITS):
                up(u)
        for m in range(KT):
            mix.add("dve", f"y{m}", (f"down{len(UNITS) - 1}",), lambda v, col, m=m: v.scalar_tensor_tensor(
                y[:, m], acc[:, m], 1.0 / 3.0, x2[:, m], ALU.mult, ALU.add))

        END = T + MLAG + 1

        def run(eng, slots_of):
            slots_of(eng, 0, 2 * BODY, 0)
            with eng.Fori(0, T // BODY - 2) as k:
                slots_of(eng, 2 * BODY, BODY, k * (BODY * B))
            slots_of(eng, T, END - T, 0)

        block = ctx.enter_context(nc.Block())
        NSET = 4 + 7 * 2

        @block.sync
        def _(sp):
            for t, name in first_loads:
                sp.dma_start(t[:], a[name]).then_inc(s_ld, 16)
            sp.dma_start(x_t[:], a["x_t"]).then_inc(s_xld, 16)
            for t, name in gru_loads:
                sp.dma_start(t[:], a[name]).then_inc(s_bld, 16)
            for l in range(2):
                sp.wait_ge(s_set, NSET)
                sp.dma_start(w_b[l][0:1, :, U:NGATE * U], a[f"b_x{l}"]).then_inc(s_bld, 16)
                sp.dma_start(w_b[l][1:2, :, 0:3 * U], a[f"b_h{l}"]).then_inc(s_bld, 16)
            for t, name in late_loads:
                sp.dma_start(t[:], a[name]).then_inc(s_mld, 16)
            run(sp, sp_slots)

        @block.tensor
        def _(pe):
            pe.wait_ge(s_ld, 16 * len(first_loads))
            for m in range(KT):
                for kt in range(KT):
                    pe.matmul(banks[0][:, B * m:B * m + B], feature_tile(w_gate[:, kt], m), cond[:, kt, :],
                              start=(kt == 0), stop=(kt == KT - 1))
            for kt in range(KT):
                mm = pe.matmul(banks[1][0:E, 0:B], w_r[:, KT + kt, :], cond[:, kt, :], start=(kt == 0), stop=(kt == KT - 1))
            mm.then_inc(s_cps, 1)
            pe.wait_ge(s_xld, 16)
            for i in range(NTB * KT):
                nb, m = divmod(i, KT)
                if i >= 4:
                    pe.wait_ge(s_mix, B * (i - 3))
                for kt in range(KT):
                    mm = pe.matmul(banks[4 + i % 4][:], feature_tile(w_in[:, kt], m), x_t[:, kt, nb * TB:(nb + 1) * TB],
                                   start=(kt == 0), stop=(kt == KT - 1))
                mm.then_inc(s_mps, 1)
            pe.wait_ge(s_bld, 16 * (len(gru_loads) + 4))
            pe.wait_ge(s_gate, KT + 1)
            pe.wait_ge(s_stg, 1)
            for piece in range(3):
                project(pe, 0, 0, piece, s_x0 if piece == 2 else None)
            pe.wait_ge(s_mix, B * NTB * KT)
            pe.wait_ge(s_pick, 1)
            pe.wait_ge(s_mld, 16 * len(late_loads))
            run(pe, pe_slots)

        @block.vector
        def _(v):
            v.memset(ones[:], 1.0).then_inc(s_set, 1)
            v.memset(pick[:], 0.0).then_inc(s_set, 1)
            v.memset(scores[:], 0.0).then_inc(s_set, 1)
            v.memset(comb[:], 0.0).then_inc(s_set, 1)
            for l in range(2):
                v.memset(w_b[l][:], 0.0).then_inc(s_set, 1)
                v.memset(slots[l][:], 0.0).then_inc(s_set, 1)
                v.memset(r_first[l][:, :, :, :, 0], 0.0).then_inc(s_set, 1)
                v.memset(r_first[l][:, :, :, :, 1], 0.5).then_inc(s_set, 1)
                v.memset(h_first[l][:, :, 0], 0.0)
                v.memset(h_first[l][:, :, 2], 0.5).then_inc(s_set, 1)
                v.memset(h_second[l][:, :, 2], 0.0).then_inc(s_set, 1)
                for p in range(2):
                    last = v.memset(r_second[l][p][:, :, :, 1], 0.5)
                last.then_inc(s_set, 1)
            for e in range(E):
                for o in range(E):
                    v.memset(lower[:, e, o:o + 1], 1.0 if o < e else 0.0)
            v.memset(mixed[:, :, T * B:], 0.0)
            v.wait_ge(s_ld, 16 * len(first_loads))
            v.tensor_scalar(b_gate_half[:], b_gate[:], 0.5, None, ALU.mult)
            for b in range(B):
                last = v.tensor_tensor(in_bias[:, :, b], b_in[:], cond[:, :, b], ALU.add)
            last.then_inc(s_bias, 1)
            v.wait_ge(s_gate, KT + 1)
            v.tensor_scalar(gate1[:], gate_th[:], 0.5, 1.5, ALU.mult, ALU.add).then_inc(s_bias, 1)
            v.wait_ge(s_x0, 1)
            turn_xn(v, 0, 0)
            run(v, dve_slots)

        @block.scalar
        def _(act):
            act.wait_ge(s_bias, 1)
            act.wait_ge(s_cps, 1)
            for m in range(KT):
                act.activation(gate_th[:, m, :], banks[0][:, B * m:B * m + B], ACT.Tanh, bias=b_gate_half[:, m:m + 1], scale=0.5)\
                   .then_inc(s_gate, 1)
            act.activation(r_bias[:], banks[1][0:E, 0:B], ACT.Identity, scale=0.5).then_inc(s_gate, 1)
            for i in range(NTB * KT):
                nb, m = divmod(i, KT)
                act.wait_ge(s_mps, i + 1)
                for b in range(B):
                    act.activation(mixed[:, m, nb * TB + b:(nb + 1) * TB:B], banks[4 + i % 4][:, b::B], ACT.Tanh,
                                   bias=in_bias[:, m, b:b + 1]).then_inc(s_mix, 1)
            act.wait_ge(s_gate, KT + 1)
            run(act, act_slots)

        @block.gpsimd
        def _(pool):
            pool.wait_ge(s_set, NSET)
            pool.affine_select(out=pick[:], in_=pick[:], compare_op=ALU.not_equal, fill=1.0, base=0,
                               pattern=[[-1, E], [0, P]], channel_multiplier=1).then_inc(s_pick, 1)
            pool.wait_ge(s_mix, B * KT)
            pool.tensor_copy(stage[0][:], mixed[:, :, 0:ROWS]).then_inc(s_stg, 1)
            pool.wait_ge(s_bias, 2)
            pool.wait_ge(s_x0, 1)
            pool.wait_ge(s_mix, B * NTB * KT)
            run(pool, pool_slots)


def _gate_columns(w, order):
    import numpy as np
    g = w.reshape((3, NQ, U) + w.shape[1:])
    g = np.stack([g[i] for i in order], axis=1)
    return np.moveaxis(g.reshape((NQ, 3 * U) + w.shape[1:]), (0, 1), (-2, -1))


def _state_rows(w):
    return w.reshape((NQ, UB, 32) + w.shape[1:]).swapaxes(1, 2).reshape((P, KT) + w.shape[1:])


def _rows(w):
    return w.reshape((-1, P) + w.shape[1:]).swapaxes(0, 1)


def kernel(**inputs):
    import numpy as np
    import concourse.bacc as bacc
    from concourse.bass_utils import run_bass_kernel_spmd

    i = {k: np.asarray(v) for k, v in inputs.items()}
    R, Z, N = 0, 1, 2
    tok = lambda v: v.transpose(2, 1, 0).reshape(D, T * B)
    arrays = {
        "x_t": _rows(tok(i["x"])), "cond": _rows(i["cond_1024"].T),
        "w_in": _rows(i["L0_cond_W_in"].T), "b_in": _rows(i["L0_cond_b_in"]),
        "w_out": _state_rows(i["L0_cond_W_out"].T), "b_out": _rows(i["L0_cond_b_out"]),
        "w_gate": _rows(_state_rows(i["L0_cond_W_gate"]).swapaxes(0, 1).reshape(D, D).T),
        "b_gate": _state_rows(i["L0_cond_b_gate"]),
        "w_r": _rows(i["L1_cond_router_W"]), "b_r": i["L1_cond_router_bias"].reshape(E, 1),
        "w_1": _rows(i["L1_cond_w1"]), "w_3": _rows(i["L1_cond_w3"]), "w_2": _rows(i["L1_cond_w2"]),
        "w_1e": i["L1_cond_W1e"].reshape(E, KT, P, HE).transpose(2, 0, 1, 3),
        "w_2e": i["L1_cond_W2e"].reshape(E, KT, P, D).transpose(2, 0, 1, 3),
    }
    for l in range(2):
        rows = _state_rows if l else _rows
        arrays[f"w_x{l}"] = rows(_gate_columns(i[f"L0_cond_Wih{l}"], (Z, R, N)))
        arrays[f"w_h{l}"] = _state_rows(_gate_columns(i[f"L0_cond_Whh{l}"], (N, Z, R)))
        arrays[f"b_x{l}"] = _gate_columns(i[f"L0_cond_bih{l}"], (Z, R, N))[None]
        arrays[f"b_h{l}"] = _gate_columns(i[f"L0_cond_bhh{l}"], (N, Z, R))[None]
    arrays = {k: np.ascontiguousarray(v) for k, v in arrays.items()}

    nc = bacc.Bacc("TRN2", target_bir_lowering=False, num_devices=1)
    a = {k: nc.dram_tensor(f"in_{k}", v.shape, F32, kind="ExternalInput").ap() for k, v in arrays.items()}
    out = nc.dram_tensor("out_y", (P, KT, T * B), F32, kind="ExternalOutput").ap()
    gru_moe_kernel(nc, a, out)
    r = run_bass_kernel_spmd(nc, [{f"in_{k}": v for k, v in arrays.items()}], core_ids=[0])
    y = r.results[0]["out_y"]
    return y.reshape(P, KT, T, B).transpose(3, 2, 1, 0).reshape(B, T, D)
```

```python
from contextlib import ExitStack

import concourse.bass as bass
from concourse import mybir
from concourse.alu_op_type import AluOpType as ALU

ACT = mybir.ActivationFunctionType
AX = mybir.AxisListType
F32 = mybir.dt.float32

P = 128
B, T, D = 2, 1024, 256
KT = D // P
NQ = 4
U = D // NQ
UB = U // 32
NGATE = 4
CH = 16
ROWS = CH * B
BODY = 4 * CH
LAG = CH + 3
ELT = 3
PITCH = ROWS * UB * ELT
OWN = B * UB * ELT
DIAG = PITCH + OWN
HS, E, HE = 512, 8, 256
TB = 512
TG = BODY * B
MLAG = BODY + LAG + 4
SH = HS // P
UNITS = [("s", i) for i in range(SH)] + [("e", i) for i in range(E)]
TSTEP = 2 * BODY
HALF = TSTEP // 2

GATES_STEP = {"r_t": 1, "hnz_t": 3, "r": 4, "z": 5, "all": 8}
STATE_STEP = ("pre_n", "h")


def gates_at(j, what):
    return GATES_STEP["all"] * j + GATES_STEP[what]


def state_at(j, what):
    return len(STATE_STEP) * j + STATE_STEP.index(what) + 1


def bias_placed(j):
    assert BIAS_STEPS[-1] + 1 < j
    return state_at(BIAS_STEPS[-1] + 1, "h")


BIAS_STEPS = range(1, 1 + NGATE)


def projection_pieces():
    return {8: (0, 0), 10: (0, 1), 1: (1, 0), 2: (1, 1)}


class Mixture:

    def __init__(self):
        self.ops = {k: [] for k in ("pe", "act", "dve", "pool")}
        self.when, self.value, self.engine = {}, {}, {}

    def add(self, engine, name, waits, issue, beside=False):
        pieces = projection_pieces()
        busy = lambda h: engine == "pe" and h % 2 == 0 and (h // 2 + MLAG) % CH in pieces
        last = self.ops[engine][-1][0] if self.ops[engine] else -1
        gap = lambda w: 2 if engine == "pe" and self.engine[w] in ("act", "pool") else 1
        h = max([self.when[w] + gap(w) for w in waits] + [last + (0 if beside else 1)])
        while busy(h):
            h += 1
        assert h < TSTEP, (name, h)
        done_before = [n for n, e in self.engine.items() if e == engine and self.when[n] // HALF == h // HALF]
        self.when[name], self.engine[name], self.value[name] = h, engine, len(done_before) + 1
        self.ops[engine].append((h, name, waits, issue))

    def half(self, name):
        return self.when[name] // HALF

    def total(self, engine, half):
        return sum(1 for n, e in self.engine.items() if e == engine and self.half(n) == half)

    def past_half(self, engine, half):
        mine = [o for o in self.ops[engine] if o[0] // HALF == half]
        late = [k for k, o in enumerate(mine) if any(self.half(w) != half for w in o[2])]
        if late or half == 0:
            k = max(late, default=0)
            return half, k + 1, mine[k][0]
        before = [o for o in self.ops[engine] if o[0] // HALF == half - 1]
        return half - 1, len(before), before[-1][0]

    def past_slot(self, half):
        return max(max(self.past_half(k, half)[2] for k in self.ops), half * HALF) // 2


def gru_moe_kernel(nc, a, out):
    with ExitStack() as ctx:
        def sb(name, *shape):
            return ctx.enter_context(nc.sbuf_tensor(name, list(shape), F32))

        def sem(name):
            return ctx.enter_context(nc.semaphore(name))

        w_in = sb("w_in", P, KT, D)
        w_x = [sb(f"w_x{l}", P, KT, NQ, 3 * U) for l in range(2)]
        w_h = [sb(f"w_h{l}", P, KT, NQ, 3 * U) for l in range(2)]
        w_b = [sb(f"w_b{l}", P, NQ, NGATE * U) for l in range(2)]
        biases = [sb(f"biases{l}", P, NGATE * U) for l in range(2)]
        w_out = sb("w_out", P, KT, D)
        w_gate = sb("w_gate", P, KT, D)
        w_r = sb("w_r", P, 2 * KT, E)
        w_1 = sb("w_1", P, KT, HS)
        w_3 = sb("w_3", P, KT, HS)
        w_2 = sb("w_2", P, SH, D)
        w_1e = sb("w_1e", P, E, KT, HE)
        w_2e = sb("w_2e", P, E, KT, D)
        b_in = sb("b_in", P, KT)
        b_out = sb("b_out", P, KT)
        b_gate = sb("b_gate", P, KT)
        b_r = sb("b_r", E, 1)
        cond = sb("cond", P, KT, B)
        ones = sb("ones", P, ROWS)
        x_t = sb("x_t", P, KT, T * B)
        mixed = sb("mixed", P, KT, T * B + ROWS)
        hist = sb("hist", P, KT, ROWS + T * B)
        in_bias = sb("in_bias", P, KT, B)
        gate_th = sb("gate_th", P, KT, B)
        gate1 = sb("gate1", P, KT, B)
        b_gate_half = sb("b_gate_half", P, KT)
        r_bias = sb("r_bias", E, B)
        stage = [sb(f"stage{l}", P, KT, ROWS) for l in range(2)]
        slots = [sb(f"slots{l}", P, CH * DIAG) for l in range(2)]
        r_pre = [sb(f"r_pre{l}", P, ROWS, UB) for l in range(2)]
        r_first = [sb(f"r_first{l}", P, 2, ROWS, UB, ELT) for l in range(2)]
        r_second = [[sb(f"r_second{l}_{p}", P, ROWS, UB, ELT) for p in range(2)] for l in range(2)]
        n_scan = [sb(f"n_scan{l}", P, B * UB, ELT) for l in range(2)]
        h_first = [sb(f"h_first{l}", P, B * UB, ELT) for l in range(2)]
        h_second = [sb(f"h_second{l}", P, B * UB, ELT) for l in range(2)]
        z_th = [sb(f"z_th{l}", P, B * UB) for l in range(2)]
        gated = sb("gated", P, KT, TG)
        x2 = sb("x2", P, KT, TG)
        y = sb("y", P, KT, TG)
        NB = TG // 32
        score_th = sb("score_th", E, TG)
        scores = sb("scores", 32, 2, TG)
        by_tok = sb("by_tok", 32, 2, NB, 32)
        gt = sb("gt", 32, NB, E, E)
        ge = sb("ge", 32, NB, E, E)
        lower = sb("lower", 32, E, E)
        rank = sb("rank", 32, NB, E)
        mask = sb("mask", 32, NB, E)
        sel = sb("sel", 32, NB, E)
        denom = sb("denom", 32, NB)
        big = sb("big", 32, NB)
        recip = sb("recip", 32, NB)
        tie = sb("tie", 32, NB)
        comb = sb("comb", 32, NB, 32)
        comb_t = sb("comb_t", 32, TG)
        pick = sb("pick", 32, E, P)
        c_all = sb("c_all", P, E, TG)
        act_t = [sb(f"act_t{i}", P, KT, TG) for i in range(2)]
        mid = sb("mid", P, 2, TG)
        hid = [sb(f"hid{i}", P, KT, TG) for i in range(2)]

        banks = [ctx.enter_context(nc.psum_tensor(f"bank{i}", [P, 512], F32)) for i in range(8)]
        gates = [[banks[2 * l + p] for p in range(2)] for l in range(2)]
        acc = banks[4][:, 0:KT * TG].rearrange("p (m n) -> p m n", m=KT)
        ups = [banks[5 + i][:, 0:2 * TG].rearrange("p (m n) -> p m n", m=2) for i in range(2)]
        misc = banks[7][:, :].rearrange("p (m n) -> p m n", n=TG)

        s_ld = sem("s_ld")
        s_xld = [sem(f"s_xld{i}") for i in range(B * T // TB)]
        s_bld = sem("s_bld")
        s_wld = [sem(f"s_wld{l}") for l in range(2)]
        s_mld = sem("s_mld")
        s_set = sem("s_set")
        s_bias = sem("s_bias")
        s_pick = sem("s_pick")
        s_mps = sem("s_mps")
        s_cps = sem("s_cps")
        s_mix = sem("s_mix")
        s_gate = sem("s_gate")
        s_stg = sem("s_stg")
        s_bps = sem("s_bps")
        s_bsb = sem("s_bsb")
        s_x0 = sem("s_x0")
        s_hist = sem("s_hist")
        KINDS = ("pe", "gates", "state", "pool", "x", "xn", "go")
        sets = [[{k: sem(f"s_{k}{l}_{p}") for k in KINDS} for p in range(2)] for l in range(2)]
        m_sets = [{k: sem(f"m_{k}_{p}") for k in ("pe", "dve", "act", "pool", "out", "go")} for p in range(2)]

        def numbers(semaphores):
            nums = [s.num for s in semaphores.values()]
            assert nums == list(range(nums[0], nums[0] + len(nums)))
            return range(nums[0], nums[0] + len(nums))

        first_loads = [(w_in, "w_in"), (b_in, "b_in"), (cond, "cond"), (w_gate, "w_gate"), (b_gate, "b_gate"), (w_r, "w_r")]
        gru_loads = [[(w_x[l], f"w_x{l}"), (w_h[l], f"w_h{l}")] for l in range(2)]
        late_loads = [(w_out, "w_out"), (w_1, "w_1"), (w_3, "w_3"), (w_2, "w_2"), (w_1e, "w_1e"), (w_2e, "w_2e"),
                      (b_out, "b_out"), (b_r, "b_r")]
        NTB = B * T // TB

        def load_x(sp, nb):
            sp.dma_start(x_t[:, :, nb * TB:(nb + 1) * TB], a["x_t"][:, :, nb * TB:(nb + 1) * TB]).then_inc(s_xld[nb], 16)

        def triples(tile):
            return tile[:].rearrange("p c e -> p (c e)")

        def own_rows(tile, j):
            return tile[:, B * j:B * j + B].rearrange("p i b e -> p (i b) e")

        def slot_state(l, j):
            return slots[l][:, j * DIAG:j * DIAG + OWN].rearrange("p (c e) -> p c e", e=ELT)

        def slot_tile(l, j, kt):
            at = j * PITCH + kt * ELT + ELT - 1
            step = UB * ELT
            return slots[l][:, at:at + (B * (j + 1) - 1) * step + 1:step]

        def schedule(s0, n):
            for s in range(s0, s0 + n):
                yield s, (s if s < T else None), (s - LAG if 0 <= s - LAG < T else None)

        def mixing_at(s):
            i, kt = divmod(s - 1, KT)
            return (KT + i, kt) if s >= 1 and KT + i < NTB * KT else None

        def mix_input(pe, i, kt):
            nb, m = divmod(i, KT)
            if kt == 0:
                if m == 0:
                    pe.wait_ge(s_xld[nb], 16)
                if i >= 4:
                    pe.wait_ge(s_mix, B * (i - 3))
            mm = pe.matmul(banks[4 + i % 4][:], w_in[:, kt, m * P:(m + 1) * P], x_t[:, kt, nb * TB:(nb + 1) * TB],
                           start=(kt == 0), stop=(kt == KT - 1))
            if kt == KT - 1:
                mm.then_inc(s_mps, 1)

        def place_biases(pe, l):
            for p in range(2):
                for g in range(NQ):
                    mm = pe.matmul(gates[l][p][32 * g:32 * g + 32, 0:NGATE * U], ones[:, :], w_b[l][:, g, :], start=True, stop=False,
                                   tile_position=(0, 32 * g), skip_group_check=True)
            mm.then_inc(s_bps, 1)

        def project(pe, l, p, kt, last=None):
            for g in range(NQ):
                mm = pe.matmul(gates[l][p][32 * g:32 * g + 32, U:NGATE * U], stage[l][:, kt, :], w_x[l][:, kt, g, :],
                               start=False, stop=False, tile_position=(0, 32 * g), skip_group_check=True)
            if last is not None:
                mm.then_inc(last, 1)

        def recur(pe, l, t):
            p, j = t // CH % 2, t % CH
            s = sets[l][p]
            if j:
                pe.wait_ge(s["state"], state_at(j - 1, "h"))
            elif t >= CH:
                pe.wait_ge(sets[l][1 - p]["state"], state_at(CH - 1, "h"))
            if j == 0:
                pe.wait_ge(sets[l][1 - p]["xn"], 1)
            if j == CH - 1 and t < T - 1:
                pe.wait_ge(s["go"], 1)
            for kt in range(KT):
                for g in range(NQ):
                    mm = pe.matmul(gates[l][p][32 * g:32 * g + B * (j + 1), 0:3 * U], slot_tile(l, j, kt), w_h[l][:, kt, g, :],
                                   start=False, stop=False, tile_position=(0, 32 * g), skip_group_check=True)
            mm.then_inc(s["pe"], 1)

        def pe_slots(pe, s0, n, base):
            for s, t0, t1 in schedule(s0, n):
                c, j = divmod(s, CH)
                p = c % 2
                if t0 is not None:
                    recur(pe, 0, t0)
                if mixing_at(s):
                    mix_input(pe, *mixing_at(s))
                l, kt = projection_pieces().get(j, (None, None))
                if l == 1 and CH <= s < T + CH:
                    if kt == 0:
                        pe.wait_ge(sets[0][p]["pool"], 1)
                        if c == 1:
                            pe.wait_ge(s_wld[1], 16 * len(gru_loads[1]))
                        if c > 2:
                            pe.wait_ge(sets[1][p]["state"], bias_placed(j + CH - LAG % CH))
                    project(pe, 1, 1 - p, kt, sets[1][p]["x"] if kt == KT - 1 else None)
                if l == 0 and t0 is not None:
                    if kt == 0:
                        pe.wait_ge(sets[0][p]["pool"], 2)
                        if c:
                            pe.wait_ge(sets[0][p]["state"], bias_placed(j))
                    project(pe, 0, 1 - p, kt, sets[0][p]["x"] if kt == KT - 1 else None)
                mixture_at(pe, "pe", s, 0, base)
                if t1 is not None:
                    recur(pe, 1, t1)
                mixture_at(pe, "pe", s, 1, base)

        def blocks(ap):
            return ap.rearrange("p (b i) -> p b i", i=32)

        def turn_xn(v, l, p):
            v.transpose(r_second[l][p][:, :, :, ELT - 1].rearrange("p i b -> p b i"),
                        blocks(gates[l][p][:, 3 * U:4 * U])).then_inc(sets[l][1 - p]["xn"], 1)

        def dve_turn(v, l, t):
            p, j = t // CH % 2, t % CH
            s = sets[l][p]
            v.wait_ge(s["pe"], j + 1)
            if j == 0:
                v.wait_ge(sets[l][1 - p]["xn"], 1)
            if j == CH - 1 and t < T - 1:
                v.wait_ge(s["go"], 1)
            v.transpose(r_pre[l][:].rearrange("p i b -> p b i"), blocks(gates[l][p][:, 2 * U:3 * U])).then_inc(s["gates"], 1)
            v.transpose(r_first[l][:].rearrange("p g i b e -> p e g b i")[:, ELT - 1],
                        gates[l][p][:, 0:2 * U].rearrange("p (g b i) -> p g b i", g=2, i=32)).then_inc(s["gates"], 2)

        def dve_n(v, l, t):
            p, j = t // CH % 2, t % CH
            s = sets[l][p]
            v.wait_ge(s["gates"], gates_at(j, "r"))
            v.tensor_tensor_scan(triples(n_scan[l]), own_rows(r_first[l][:, 0], j).rearrange("p c e -> p (c e)"),
                                 own_rows(r_second[l][p], j).rearrange("p c e -> p (c e)"), 0.0, ALU.mult, ALU.add)\
                .then_inc(s["state"], 1)
            v.wait_ge(s["gates"], gates_at(j, "z"))
            v.tensor_scalar(h_first[l][:, :, 1], z_th[l][:], -1.0, 1.0, ALU.mult, ALU.add).then_inc(s["gates"], 1)
            v.scalar_tensor_tensor(h_second[l][:, :, 1], z_th[l][:], 1.0, slot_state(l, j)[:, :, ELT - 1], ALU.add, ALU.mult)\
                .then_inc(s["gates"], 1)

        def dve_h(v, l, t):
            p, j = t // CH % 2, t % CH
            s = sets[l][p]
            v.wait_ge(s["gates"], gates_at(j, "all"))
            if j == 0:
                v.wait_ge(s["pool"], 1)
            v.tensor_tensor_scan(slot_state(l, (j + 1) % CH).rearrange("p c e -> p (c e)"), triples(h_first[l]),
                                 triples(h_second[l]), 0.0, ALU.mult, ALU.add).then_inc(s["state"], 1)

        def dve_slots(v, s0, n, base):
            for s, t0, t1 in schedule(s0, n):
                c, j = divmod(s, CH)
                p = c % 2
                if 0 <= s - 1 - LAG < T:
                    dve_h(v, 1, s - 1 - LAG)
                if t0 is not None:
                    dve_turn(v, 0, t0)
                mixture_at(v, "dve", s, 0, base)
                if t0 is not None:
                    dve_n(v, 0, t0)
                    if j == 12:
                        v.wait_ge(sets[0][p]["x"], 1)
                        turn_xn(v, 0, 1 - p)
                if CH <= s < T + CH and j == 2:
                    v.wait_ge(sets[1][p]["x"], 1)
                    turn_xn(v, 1, 1 - p)
                if t0 is not None:
                    dve_h(v, 0, t0)
                if t1 is not None:
                    dve_turn(v, 1, t1)
                mixture_at(v, "dve", s, 1, base)
                if t1 is not None:
                    dve_n(v, 1, t1)

        def act_step(act, l, t):
            p, j = t // CH % 2, t % CH
            s = sets[l][p]
            act.wait_ge(s["gates"], gates_at(j, "r_t"))
            if j == CH - 1 and t < T - 1:
                act.wait_ge(s["go"], 1)
            own = r_pre[l][:, B * j:B * j + B, :].rearrange("p i b -> p (i b)")
            act.activation(own_rows(r_second[l][p], j)[:, :, 0], own, ACT.Tanh, scale=0.5).then_inc(s["gates"], 1)
            act.wait_ge(s["gates"], gates_at(j, "hnz_t"))
            act.activation(z_th[l][:], own_rows(r_first[l][:, 1], j)[:, :, ELT - 1], ACT.Tanh, scale=0.5).then_inc(s["gates"], 1)
            act.wait_ge(s["state"], state_at(j, "pre_n"))
            act.activation(h_second[l][:, :, 0], n_scan[l][:, :, ELT - 1], ACT.Tanh).then_inc(s["gates"], 1)
            if CH <= t < T - CH and j in BIAS_STEPS:
                quarter = slice((j - BIAS_STEPS[0]) * U, (j - BIAS_STEPS[0] + 1) * U)
                act.activation(gates[l][1 - p][:, quarter], biases[l][:, quarter], ACT.Identity)

        def mixed_tanh(act, i):
            nb, m = divmod(i, KT)
            act.wait_ge(s_mps, i + 1)
            for b in range(B):
                act.activation(mixed[:, m, nb * TB + b:(nb + 1) * TB:B], banks[4 + i % 4][:, b::B], ACT.Tanh,
                               bias=in_bias[:, m, b:b + 1]).then_inc(s_mix, 1)

        def act_slots(act, s0, n, base):
            for s, t0, t1 in schedule(s0, n):
                if t0 is not None:
                    act_step(act, 0, t0)
                if mixing_at(s - 1) and mixing_at(s - 1)[1] == KT - 1:
                    mixed_tanh(act, mixing_at(s - 1)[0])
                mixture_at(act, "act", s, 0, base)
                if t1 is not None:
                    act_step(act, 1, t1)
                mixture_at(act, "act", s, 1, base)

        def read_out(pool, l, dst, done):
            by = slots[l][:].rearrange("p (j r) -> p j r", r=DIAG)
            view = dst.rearrange("p k (j b) -> p k j b", b=B)
            for kt in range(KT):
                own = by[:, :, 0:OWN].rearrange("p j (b k e) -> p j b k e", b=B, e=ELT)[:, :, :, kt, ELT - 1]
                pool.tensor_copy(view[:, kt, 0:CH - 1], own[:, 1:CH])
                last = pool.tensor_copy(view[:, kt, CH - 1], own[:, 0])
            last.then_inc(done, 1)

        def pool_slots(pool, s0, n, base):
            for s, t0, t1 in schedule(s0, n):
                c, j = divmod(s, CH)
                p = c % 2
                if s == CH:
                    pool.wait_ge(s_mix, B * NTB * KT)
                if j == 0 and s <= T:
                    if s >= CH:
                        pool.wait_ge(sets[0][1 - p]["go"], 1)
                        pool.wait_ge(sets[0][1 - p]["state"], state_at(CH - 1, "h"))
                    read_out(pool, 0, stage[1][:], sets[0][p]["pool"])
                    if t0 is not None:
                        pool.tensor_copy(stage[0][:], mixed[:, :, bass.ds(base + (c + 1) * ROWS, ROWS)])\
                            .then_inc(sets[0][p]["pool"], 1)
                if t1 is not None and t1 % CH == 0:
                    cb = t1 // CH
                    pb = cb % 2
                    if t1 >= CH:
                        pool.wait_ge(sets[1][1 - pb]["go"], 1)
                        pool.wait_ge(sets[1][1 - pb]["state"], state_at(CH - 1, "h"))
                    read_out(pool, 1, hist[:, :, bass.ds(base + cb * ROWS, ROWS)], sets[1][pb]["pool"])
                if s == T + LAG:
                    pool.wait_ge(sets[1][1]["state"], state_at(CH - 1, "h"))
                    read_out(pool, 1, hist[:, :, T * B:], s_hist)
                mixture_at(pool, "pool", s, 0, base)
                mixture_at(pool, "pool", s, 1, base)

        def sp_slots(sp, s0, n, base):
            for s, t0, t1 in schedule(s0, n):
                for l, t in ((0, t0), (1, t1)):
                    if t is not None and t % CH == 0:
                        p = t // CH % 2
                        now = sets[l][p]
                        sp.wait_ge(now["pe"], 1)
                        sp.wait_ge(now["gates"], gates_at(0, "r"))
                        sp.wait_ge(now["pool"], 2 - l)
                        sp.sem_clear(numbers(sets[l][1 - p]))
                        sp.sem_inc(now["go"], 1)
                m = s - MLAG
                if not 0 <= m < T:
                    continue
                for half in range(2):
                    if m % BODY != mix.past_slot(half):
                        continue
                    for k in mix.ops:
                        in_set, count, _ = mix.past_half(k, half)
                        sp.wait_ge(m_sets[in_set][k], count)
                    sp.sem_clear(numbers(m_sets[1 - half]))
                    sp.sem_inc(m_sets[half]["go"], 1)
                if m % BODY == mix.when["y1"] // 2:
                    sp.wait_ge(m_sets[1]["dve"], mix.value["y1"])
                    sp.dma_start(out[:, :, bass.ds(base + m // BODY * TG, TG)], y[:]).then_inc(m_sets[1]["out"], 16)
                    sp.wait_ge(m_sets[1]["out"], 16)

        mix = Mixture()

        def wait_for(eng, name):
            eng.wait_ge(m_sets[mix.half(name)][mix.engine[name]], mix.value[name])

        def mixture_at(eng, engine, s, part, base):
            m = s - MLAG
            if not 0 <= m < T:
                return
            group, h = m // BODY, m % BODY * 2 + part
            for at, name, waits, issue in mix.ops[engine]:
                if at != h:
                    continue
                for w in waits:
                    wait_for(eng, w)
                half = h // HALF
                if name == "out00" and group == 0:
                    eng.wait_ge(s_mld, 16 * len(late_loads))
                    eng.wait_ge(s_mix, B * NTB * KT)
                    eng.wait_ge(s_pick, 1)
                if name == "out00" and group > 0:
                    eng.wait_ge(m_sets[1]["dve"], mix.value["y1"])
                if name == "gated":
                    eng.wait_ge(*((sets[1][0]["pool"], 1) if group < T // BODY - 1 else (s_hist, 1)))
                if mix.value[name] == mix.total(engine, half) and (group, half) != (T // BODY - 1, 1):
                    eng.wait_ge(m_sets[half]["go"], 1)
                issue(eng, base + group * TG).then_inc(m_sets[half][engine], 1)

        def product(ps, w, x, start, stop):
            return lambda pe, col: pe.matmul(ps, w, x, start=start, stop=stop, skip_group_check=True)

        def feature_tile(w, m):
            return w[:, m * P:(m + 1) * P]

        gated4 = gated[:].rearrange("p k (t b) -> p k t b", b=B)
        mix.add("pool", "gated", (), lambda pool, col: pool.tensor_tensor(
            gated4, hist[:, :, bass.ds(col + ROWS, TG)].rearrange("p k (t b) -> p k t b", b=B),
            gate1[:].unsqueeze(2).to_broadcast([P, KT, BODY, B]), ALU.mult))
        for m in range(KT):
            for kt in range(KT):
                mix.add("pe", f"out{m}{kt}", ("gated",) if m == kt == 0 else (),
                        product(misc[:, m], feature_tile(w_out[:, kt], m), gated[:, kt], m == kt == 0, kt == KT - 1))
        for m in range(KT):
            mix.add("dve", f"x2{m}", (f"out{KT - 1}{KT - 1}",), lambda v, col, m=m: v.scalar_tensor_tensor(
                x2[:, m], misc[:, m], b_out[:, m:m + 1], x_t[:, m, bass.ds(col, TG)], ALU.add, ALU.add))
        for kt in range(KT):
            mix.add("pe", f"route{kt}", ("x21",), product(misc[0:E, 0], w_r[:, kt], x2[:, kt], kt == 0, kt == KT - 1), beside=kt > 0)
        for b in range(B):
            mix.add("act", f"score{b}", (f"route{KT - 1}",), lambda act, col, b=b: act.activation(
                score_th[:, b::B], misc[0:E, 0, b::B], ACT.Tanh, bias=r_bias[:, b:b + 1], scale=0.5))

        def up(u):
            kind, i = UNITS[u]
            free = () if u < 2 else (f"hid{u - 2}",)
            for h in range(2):
                for kt in range(KT):
                    if kind == "s":
                        w = feature_tile((w_1, w_3)[h][:, kt], i)
                    else:
                        w = feature_tile(w_1e[:, i, kt], h)
                    mix.add("pe", f"up{u}_{h}{kt}", free if h == kt == 0 else (),
                            product(ups[u % 2][:, h], w, x2[:, kt], h == kt == 0, kt == KT - 1))

        def nonlinear(u):
            kind, i = UNITS[u]
            bank, done = ups[u % 2], f"up{u}_{1}{KT - 1}"
            read = () if u < 2 else (f"hid{u - 2}",)
            if kind == "s":
                mix.add("act", f"act{u}", (done,) + read, lambda act, col: act.activation(
                    act_t[u % 2][:, 0], bank[:, 0], ACT.Tanh, scale=0.5))
                mix.add("dve", f"mid{u}", (f"act{u}",), lambda v, col: v.scalar_tensor_tensor(
                    mid[:, u % 2], act_t[u % 2][:, 0], 1.0, bank[:, 0], ALU.add, ALU.mult))
                freed = () if u < 2 else (f"down{u - 2}",)
                mix.add("dve", f"hid{u}", (f"mid{u}",) + freed, lambda v, col: v.scalar_tensor_tensor(
                    hid[u % 2][:, 0], mid[:, u % 2], 0.5, bank[:, 1], ALU.mult, ALU.mult))
            else:
                mix.add("act", f"act{u}", (done,) + read, lambda act, col: act.activation(
                    act_t[u % 2][:], bank[:, :], ACT.Gelu))

        def weigh(u):
            kind, i = UNITS[u]
            if kind == "e":
                mix.add("pool", f"hid{u}", (f"act{u}", f"down{u - 2}") + ((f"gates{i}",) if i < 2 else ()), lambda v, col: v.tensor_tensor(
                    hid[u % 2][:], act_t[u % 2][:], c_all[:, i].unsqueeze(1).to_broadcast([P, KT, TG]), ALU.mult))

        def down(u):
            kind, i = UNITS[u]
            tiles = [w_2[:, i]] if kind == "s" else [w_2e[:, i, kt] for kt in range(KT)]
            for k, w in enumerate(tiles):
                for m in range(KT):
                    last = k == len(tiles) - 1 and m == KT - 1
                    name = f"down{u}" if last else f"down{u}_{k}{m}"
                    mix.add("pe", name, (f"hid{u}",) if k == m == 0 else (),
                            product(acc[:, m], feature_tile(w, m), hid[u % 2][:, k], u == k == m == 0, u == len(UNITS) - 1 and last))

        mine = by_tok[:, 1, :, 0:E].unsqueeze(3).to_broadcast([32, NB, E, E])
        other = by_tok[:, 1, :, 0:E].unsqueeze(2).to_broadcast([32, NB, E, E])
        per_expert = [32, NB, E]
        flat = lambda t: t.rearrange("p n e -> p (n e)")
        ROUTE = [
            ("s", "score1", lambda v, col: v.tensor_scalar(scores[0:E, 0], score_th[:], 0.5, 0.5, ALU.mult, ALU.add)),
            ("s_bias", "s", lambda v, col: v.tensor_scalar(scores[0:E, 1], scores[0:E, 0], b_r[:, 0:1], None, ALU.add)),
            ("tok0", "s", lambda v, col: v.transpose(flat(by_tok[:, 0]), scores[:, 0])),
            ("tok1", "s_bias", lambda v, col: v.transpose(flat(by_tok[:, 1]), scores[:, 1])),
            *[(f"{name}{i}", "tok1", lambda v, col, t=t, op=op, n=slice(NB // 2 * i, NB // 2 * (i + 1)):
               v.tensor_tensor(t[:, n], other[:, n], mine[:, n], op))
              for name, t, op in (("gt", gt, ALU.is_gt), ("ge", ge, ALU.is_ge)) for i in range(2)],
            ("equal", "ge1", lambda v, col: v.tensor_tensor(ge[:], ge[:], gt[:], ALU.subtract)),
            ("before", "equal", lambda v, col: v.tensor_tensor(
                ge[:], ge[:], lower[:].unsqueeze(1).to_broadcast([32, NB, E, E]), ALU.mult)),
            ("count", "before", lambda v, col: v.tensor_tensor(gt[:], gt[:], ge[:], ALU.add)),
            ("rank4", "count", lambda v, col: v.tensor_tensor(gt[:, :, :, 0:4], gt[:, :, :, 0:4], gt[:, :, :, 4:8], ALU.add)),
            ("rank2", "rank4", lambda v, col: v.tensor_tensor(gt[:, :, :, 0:2], gt[:, :, :, 0:2], gt[:, :, :, 2:4], ALU.add)),
            ("rank", "rank2", lambda v, col: v.tensor_tensor(rank[:], gt[:, :, :, 0], gt[:, :, :, 1], ALU.add)),
            ("mask", "rank", lambda v, col: v.tensor_scalar(mask[:], rank[:], 1.5, None, ALU.is_lt)),
            ("sel", "mask", lambda v, col: v.tensor_tensor(sel[:], mask[:], by_tok[:, 0, :, 0:E], ALU.mult)),
            ("denom", "sel", lambda v, col: v.tensor_reduce(denom[:], sel[:], AX.X, ALU.add)),
            ("big", "denom", lambda v, col: v.tensor_scalar(big[:], denom[:], 1e-9, None, ALU.is_gt)),
            ("dplus", "denom", lambda v, col: v.tensor_scalar(denom[:], denom[:], 1e-9, None, ALU.add)),
            ("recip", "dplus", lambda v, col: v.reciprocal(recip[:], denom[:])),
            ("tie", "big", lambda v, col: v.tensor_scalar(tie[:], big[:], -0.5, 0.5, ALU.mult, ALU.add)),
            ("scale", "recip", lambda v, col: v.tensor_tensor(recip[:], recip[:], big[:], ALU.mult)),
            ("w_tie", "tie", lambda v, col: v.tensor_tensor(mask[:], mask[:], tie[:].unsqueeze(2).to_broadcast(per_expert), ALU.mult)),
            ("w_sel", "scale", lambda v, col: v.tensor_tensor(sel[:], sel[:], recip[:].unsqueeze(2).to_broadcast(per_expert), ALU.mult)),
            ("comb", "w_sel", lambda v, col: v.tensor_tensor(comb[:, :, 0:E], sel[:], mask[:], ALU.add)),
            ("comb_t", "comb", lambda v, col: v.transpose(comb_t[:], flat(comb[:]))),
        ]

        ON_POOL = ("equal", "before", "count", "rank4", "rank2", "rank", "sel", "scale", "w_tie", "w_sel", "comb")

        def route(n):
            for _ in range(n):
                name, after, issue = ROUTE.pop(0)
                engine = "pool" if name in ON_POOL else "dve"
                mix.add(engine, name, (after,), issue, beside=name in ("tok0", "dplus", "tie", "w_tie"))

        for u in range(SH):
            up(u)
            if u >= 1:
                nonlinear(u - 1)
            route(3)
            if u >= 2:
                down(u - 2)
        nonlinear(SH - 1)
        route(len(ROUTE))
        down(SH - 2)
        down(SH - 1)
        for q in range(2):
            up(SH + q)
        for q in range(2):
            for i in range(4):
                mix.add("pe", f"spread{q}{i}", (f"gates{q - 1}",) if q and i == 0 else ("comb_t",) if i == 0 else (),
                        product(misc[:, i], pick[:, 4 * q + i], comb_t[:], i == 0, True))
            mix.add("act", f"gates{q}", (f"spread{q}3",), lambda act, col, q=q: act.activation(
                c_all[:, 4 * q:4 * q + 4], misc[:, :], ACT.Identity))
            if q == 0:
                nonlinear(SH)
        for u in range(SH + 2, len(UNITS) + 2):
            weigh(u - 2)
            if u - 1 < len(UNITS):
                nonlinear(u - 1)
            down(u - 2)
            if u < len(UNITS):
                up(u)
        for m in range(KT):
            mix.add("dve", f"y{m}", (f"down{len(UNITS) - 1}",), lambda v, col, m=m: v.scalar_tensor_tensor(
                y[:, m], acc[:, m], 1.0 / 3.0, x2[:, m], ALU.mult, ALU.add))

        END = T + MLAG + 1

        def run(eng, slots_of):
            slots_of(eng, 0, 2 * BODY, 0)
            with eng.Fori(0, T // BODY - 2) as k:
                slots_of(eng, 2 * BODY, BODY, k * (BODY * B))
            slots_of(eng, T, END - T, 0)

        block = ctx.enter_context(nc.Block())
        NSET = 4 + 7 * 2

        @block.sync
        def _(sp):
            for t, name in first_loads:
                sp.dma_start(t[:], a[name]).then_inc(s_ld, 16)
            load_x(sp, 0)
            for t, name in gru_loads[0]:
                sp.dma_start(t[:], a[name]).then_inc(s_wld[0], 16)
            sp.wait_ge(s_set, 2)
            for l in range(2):
                sp.dma_start(w_b[l][0:1, :, U:NGATE * U], a[f"b_x{l}"]).then_inc(s_bld, 16)
                sp.dma_start(w_b[l][1:2, :, 0:3 * U], a[f"b_h{l}"]).then_inc(s_bld, 16)
            for nb in range(1, NTB):
                load_x(sp, nb)
            for t, name in gru_loads[1]:
                sp.dma_start(t[:], a[name]).then_inc(s_wld[1], 16)
            for t, name in late_loads:
                sp.dma_start(t[:], a[name]).then_inc(s_mld, 16)
            run(sp, sp_slots)

        @block.tensor
        def _(pe):
            pe.wait_ge(s_ld, 16 * len(first_loads))
            for m in range(KT):
                for kt in range(KT):
                    pe.matmul(banks[0][:, B * m:B * m + B], feature_tile(w_gate[:, kt], m), cond[:, kt, :],
                              start=(kt == 0), stop=(kt == KT - 1))
            for kt in range(KT):
                mm = pe.matmul(banks[1][0:E, 0:B], w_r[:, KT + kt, :], cond[:, kt, :], start=(kt == 0), stop=(kt == KT - 1))
            mm.then_inc(s_cps, 1)
            for i in range(KT):
                for kt in range(KT):
                    mix_input(pe, i, kt)
            pe.wait_ge(s_bld, 16 * 4)
            pe.wait_ge(s_gate, KT + 1)
            for l in range(2):
                place_biases(pe, l)
            pe.wait_ge(s_bsb, 1)
            pe.wait_ge(s_wld[0], 16 * len(gru_loads[0]))
            pe.wait_ge(s_stg, 1)
            for kt in range(KT):
                project(pe, 0, 0, kt, s_x0 if kt == KT - 1 else None)
            run(pe, pe_slots)

        @block.vector
        def _(v):
            for l in range(2):
                v.memset(w_b[l][:], 0.0).then_inc(s_set, 1)
            v.memset(ones[:], 1.0).then_inc(s_set, 1)
            v.memset(pick[:], 0.0).then_inc(s_set, 1)
            v.memset(scores[:], 0.0).then_inc(s_set, 1)
            v.memset(comb[:], 0.0).then_inc(s_set, 1)
            for l in range(2):
                v.memset(slots[l][:], 0.0).then_inc(s_set, 1)
                v.memset(r_first[l][:, :, :, :, 0], 0.0).then_inc(s_set, 1)
                v.memset(r_first[l][:, :, :, :, 1], 0.5).then_inc(s_set, 1)
                v.memset(h_first[l][:, :, 0], 0.0)
                v.memset(h_first[l][:, :, 2], 0.5).then_inc(s_set, 1)
                v.memset(h_second[l][:, :, 2], 0.0).then_inc(s_set, 1)
                for p in range(2):
                    last = v.memset(r_second[l][p][:, :, :, 1], 0.5)
                last.then_inc(s_set, 1)
            for e in range(E):
                for o in range(E):
                    v.memset(lower[:, e, o:o + 1], 1.0 if o < e else 0.0)
            v.memset(mixed[:, :, T * B:], 0.0)
            v.wait_ge(s_ld, 16 * len(first_loads))
            v.tensor_scalar(b_gate_half[:], b_gate[:], 0.5, None, ALU.mult)
            for b in range(B):
                last = v.tensor_tensor(in_bias[:, :, b], b_in[:], cond[:, :, b], ALU.add)
            last.then_inc(s_bias, 1)
            v.wait_ge(s_gate, KT + 1)
            v.tensor_scalar(gate1[:], gate_th[:], 0.5, 1.5, ALU.mult, ALU.add).then_inc(s_bias, 1)
            for l in range(2):
                v.wait_ge(s_bps, l + 1)
                v.tensor_copy(biases[l][:], gates[l][0][:, 0:NGATE * U]).then_inc(s_bsb, 1)
            v.wait_ge(s_x0, 1)
            turn_xn(v, 0, 0)
            run(v, dve_slots)

        @block.scalar
        def _(act):
            act.wait_ge(s_bias, 1)
            act.wait_ge(s_cps, 1)
            for m in range(KT):
                act.activation(gate_th[:, m, :], banks[0][:, B * m:B * m + B], ACT.Tanh, bias=b_gate_half[:, m:m + 1], scale=0.5)\
                   .then_inc(s_gate, 1)
            act.activation(r_bias[:], banks[1][0:E, 0:B], ACT.Identity, scale=0.5).then_inc(s_gate, 1)
            for i in range(KT):
                mixed_tanh(act, i)
            act.wait_ge(s_gate, KT + 1)
            run(act, act_slots)

        @block.gpsimd
        def _(pool):
            pool.wait_ge(s_set, NSET)
            pool.affine_select(out=pick[:], in_=pick[:], compare_op=ALU.not_equal, fill=1.0, base=0,
                               pattern=[[-1, E], [0, P]], channel_multiplier=1).then_inc(s_pick, 1)
            pool.wait_ge(s_mix, B * KT)
            pool.tensor_copy(stage[0][:], mixed[:, :, 0:ROWS]).then_inc(s_stg, 1)
            pool.wait_ge(s_bias, 2)
            pool.wait_ge(s_x0, 1)
            run(pool, pool_slots)


def _gate_columns(w, order):
    import numpy as np
    g = w.reshape((3, NQ, U) + w.shape[1:])
    g = np.stack([g[i] for i in order], axis=1)
    return np.moveaxis(g.reshape((NQ, 3 * U) + w.shape[1:]), (0, 1), (-2, -1))


def _state_rows(w):
    return w.reshape((NQ, UB, 32) + w.shape[1:]).swapaxes(1, 2).reshape((P, KT) + w.shape[1:])


def _rows(w):
    return w.reshape((-1, P) + w.shape[1:]).swapaxes(0, 1)


def kernel(**inputs):
    import numpy as np
    import concourse.bacc as bacc
    from concourse.bass_utils import run_bass_kernel_spmd

    i = {k: np.asarray(v) for k, v in inputs.items()}
    R, Z, N = 0, 1, 2
    tok = lambda v: v.transpose(2, 1, 0).reshape(D, T * B)
    arrays = {
        "x_t": _rows(tok(i["x"])), "cond": _rows(i["cond_1024"].T),
        "w_in": _rows(i["L0_cond_W_in"].T), "b_in": _rows(i["L0_cond_b_in"]),
        "w_out": _state_rows(i["L0_cond_W_out"].T), "b_out": _rows(i["L0_cond_b_out"]),
        "w_gate": _rows(_state_rows(i["L0_cond_W_gate"]).swapaxes(0, 1).reshape(D, D).T),
        "b_gate": _state_rows(i["L0_cond_b_gate"]),
        "w_r": _rows(i["L1_cond_router_W"]), "b_r": i["L1_cond_router_bias"].reshape(E, 1),
        "w_1": _rows(i["L1_cond_w1"]), "w_3": _rows(i["L1_cond_w3"]), "w_2": _rows(i["L1_cond_w2"]),
        "w_1e": i["L1_cond_W1e"].reshape(E, KT, P, HE).transpose(2, 0, 1, 3),
        "w_2e": i["L1_cond_W2e"].reshape(E, KT, P, D).transpose(2, 0, 1, 3),
    }
    for l in range(2):
        rows = _state_rows if l else _rows
        arrays[f"w_x{l}"] = rows(_gate_columns(i[f"L0_cond_Wih{l}"], (Z, R, N)))
        arrays[f"w_h{l}"] = _state_rows(_gate_columns(i[f"L0_cond_Whh{l}"], (N, Z, R)))
        arrays[f"b_x{l}"] = _gate_columns(i[f"L0_cond_bih{l}"], (Z, R, N))[None]
        arrays[f"b_h{l}"] = _gate_columns(i[f"L0_cond_bhh{l}"], (N, Z, R))[None]
    arrays = {k: np.ascontiguousarray(v) for k, v in arrays.items()}

    nc = bacc.Bacc("TRN2", target_bir_lowering=False, num_devices=1)
    a = {k: nc.dram_tensor(f"in_{k}", v.shape, F32, kind="ExternalInput").ap() for k, v in arrays.items()}
    out = nc.dram_tensor("out_y", (P, KT, T * B), F32, kind="ExternalOutput").ap()
    gru_moe_kernel(nc, a, out)
    r = run_bass_kernel_spmd(nc, [{f"in_{k}": v for k, v in arrays.items()}], core_ids=[0])
    y = r.results[0]["out_y"]
    return y.reshape(P, KT, T, B).transpose(3, 2, 1, 0).reshape(B, T, D)
```
